# Optimizing a Trainium2 kernel written in Bass

```python
import numpy as np
import jax
import jax.numpy as jnp

def _softmax(x, axis=-1):
    return jax.nn.softmax(x, axis=axis)

def _gelu(x):
    return jax.nn.gelu(x, approximate=True)

def _silu(x):
    return jax.nn.silu(x)

def _sigmoid(x):
    return jax.nn.sigmoid(x)

def _layernorm(x, axis=-1, eps=1e-05):
    m = jnp.mean(x, axis=axis, keepdims=True)
    v = jnp.var(x, axis=axis, keepdims=True)
    return (x - m) / jnp.sqrt(v + eps)

def _scatter_add(tgt, idx, src, axis=0):
    return tgt.at[idx].add(src)

def _segment_sum(src, seg, n):
    return jax.ops.segment_sum(src, seg, n)
kernel_name = 'mk_early_fusion_d1_tok_img1024_r4_62aada'

def setup_inputs(seed: int=0):
    np.random.seed(seed)
    _w = jnp.asarray

    def _rec_inputs():
        import jax
        import jax.numpy as jnp
        _rk = jax.random.key(seed)
        x = -0.00016672 + 0.999947 * jax.random.normal(jax.random.fold_in(_rk, 1), (64, 3, 224, 224), jnp.float32)
        txt = 0.435037 + 1.14557 * jax.random.normal(jax.random.fold_in(_rk, 2), (64, 77, 256), jnp.float32)
        return (x, txt)
    x, txt = _rec_inputs()

    def _L0_tok_setup():
        import jax, jax.numpy as jnp
        import numpy as np
        PATCH = 16
        EPS = 1e-05

        def _patchify(img, p):
            B, C, H, W = img.shape
            h, w = (H // p, W // p)
            x = img.reshape(B, C, h, p, w, p)
            x = x.transpose(0, 2, 4, 1, 3, 5)
            return x.reshape(B, h, w, C * p * p)

        def _layernorm(x, gamma):
            mu = x.mean(axis=-1, keepdims=True)
            var = ((x - mu) ** 2).mean(axis=-1, keepdims=True)
            return (x - mu) * jax.lax.rsqrt(var + EPS) * gamma

        def _posemb_sincos_2d(h, w, dim, temperature=10000.0, dtype=jnp.float32):
            y, x = jnp.meshgrid(jnp.arange(h, dtype=dtype), jnp.arange(w, dtype=dtype), indexing='ij')
            omega = jnp.arange(dim // 4, dtype=dtype) / (dim // 4 - 1)
            omega = 1.0 / temperature ** omega
            y = y.reshape(-1)[:, None] * omega[None, :]
            x = x.reshape(-1)[:, None] * omega[None, :]
            return jnp.concatenate([jnp.sin(x), jnp.cos(x), jnp.sin(y), jnp.cos(y)], axis=1)
        key = jax.random.key(seed)
        k1, k2, k3, k4 = jax.random.split(key, 4)
        patch_dim = 3 * PATCH * PATCH
        dim = 256
        img = jax.random.normal(k1, (64, 3, 96, 96), dtype=jnp.float32)
        ln1_w = jax.random.uniform(k2, (patch_dim,), dtype=jnp.float32, minval=0.9, maxval=1.1)
        W = jax.random.normal(k3, (dim, patch_dim), dtype=jnp.float32) * 0.02
        ln2_w = jax.random.uniform(k4, (dim,), dtype=jnp.float32, minval=0.9, maxval=1.1)
        return {'img': img, 'ln1_w': ln1_w, 'W': W, 'ln2_w': ln2_w}
    _L0_tok_all = _L0_tok_setup()
    _L0_tok_in = {k: v for k, v in _L0_tok_all.items() if k in ('ln1_w', 'W', 'ln2_w')}
    del _L0_tok_all

    def _L0_attn_setup():
        import jax, jax.numpy as jnp
        import numpy as np
        EPS = 1e-05

        def _apply_rope(t, cos, sin):
            B, H, S, D = t.shape
            tr = t.reshape(B, H, S, D // 2, 2)
            x0, x1 = (tr[..., 0], tr[..., 1])
            r0 = x0 * cos - x1 * sin
            r1 = x0 * sin + x1 * cos
            return jnp.stack([r0, r1], axis=-1).reshape(B, H, S, D)
        key = jax.random.key(seed)
        ks = jax.random.split(key, 3)
        B, S, DM = (2, 512, 256)
        return {'x': jax.random.normal(ks[0], (B, S, DM), jnp.float32), 'Wqkv': jax.random.normal(ks[1], (DM, 3 * DM), jnp.float32) * 0.02, 'bqkv': jnp.zeros((3 * DM,), jnp.float32), 'Wo': jax.random.normal(ks[2], (DM, DM), jnp.float32) * 0.02, 'bo': jnp.zeros((DM,), jnp.float32), 'gamma': jnp.ones((DM,), jnp.float32), 'beta': jnp.zeros((DM,), jnp.float32)}
    _L0_attn_all = _L0_attn_setup()
    _L0_attn_in = {k: v for k, v in _L0_attn_all.items() if k in ('Wqkv', 'bqkv', 'Wo', 'bo', 'gamma', 'beta')}
    del _L0_attn_all

    def _L0_ffn_setup():
        import math
        import jax, jax.numpy as jnp
        import numpy as np
        B, S, D, F, E = (8, 512, 256, 1024, 8)
        CAPACITY_FACTOR = 1.0
        key = jax.random.key(seed)
        k1, k2, k3, k4 = jax.random.split(key, 4)
        x = jax.random.normal(k1, (B, S, D), dtype=jnp.float32)
        Wr = jax.random.normal(k2, (D, E), dtype=jnp.float32) * (1.0 / math.sqrt(D))
        W1 = jax.random.normal(k3, (E, D, F), dtype=jnp.float32) * (1.0 / math.sqrt(D))
        W2 = jax.random.normal(k4, (E, F, D), dtype=jnp.float32) * (1.0 / math.sqrt(F))
        return {'x': x, 'Wr': Wr, 'W1': W1, 'W2': W2}
    _L0_ffn_all = _L0_ffn_setup()
    _L0_ffn_in = {k: v for k, v in _L0_ffn_all.items() if k in ('Wr', 'W1', 'W2')}
    del _L0_ffn_all
    return {'x': x, 'txt': txt, 'L0_tok_ln1_w': _L0_tok_in['ln1_w'], 'L0_tok_W': _L0_tok_in['W'], 'L0_tok_ln2_w': _L0_tok_in['ln2_w'], 'L0_attn_Wqkv': _L0_attn_in['Wqkv'], 'L0_attn_bqkv': _L0_attn_in['bqkv'], 'L0_attn_Wo': _L0_attn_in['Wo'], 'L0_attn_bo': _L0_attn_in['bo'], 'L0_attn_gamma': _L0_attn_in['gamma'], 'L0_attn_beta': _L0_attn_in['beta'], 'L0_ffn_Wr': _L0_ffn_in['Wr'], 'L0_ffn_W1': _L0_ffn_in['W1'], 'L0_ffn_W2': _L0_ffn_in['W2']}

def reference(x, txt, L0_tok_ln1_w, L0_tok_W, L0_tok_ln2_w, L0_attn_Wqkv, L0_attn_bqkv, L0_attn_Wo, L0_attn_bo, L0_attn_gamma, L0_attn_beta, L0_ffn_Wr, L0_ffn_W1, L0_ffn_W2):
    import jax
    import jax.numpy as jnp

    def _L0_tok_ref(img, ln1_w, W, ln2_w):
        import jax, jax.numpy as jnp
        import numpy as np
        PATCH = 16
        EPS = 1e-05

        def _patchify(img, p):
            B, C, H, W = img.shape
            h, w = (H // p, W // p)
            x = img.reshape(B, C, h, p, w, p)
            x = x.transpose(0, 2, 4, 1, 3, 5)
            return x.reshape(B, h, w, C * p * p)

        def _layernorm(x, gamma):
            mu = x.mean(axis=-1, keepdims=True)
            var = ((x - mu) ** 2).mean(axis=-1, keepdims=True)
            return (x - mu) * jax.lax.rsqrt(var + EPS) * gamma

        def _posemb_sincos_2d(h, w, dim, temperature=10000.0, dtype=jnp.float32):
            y, x = jnp.meshgrid(jnp.arange(h, dtype=dtype), jnp.arange(w, dtype=dtype), indexing='ij')
            omega = jnp.arange(dim // 4, dtype=dtype) / (dim // 4 - 1)
            omega = 1.0 / temperature ** omega
            y = y.reshape(-1)[:, None] * omega[None, :]
            x = x.reshape(-1)[:, None] * omega[None, :]
            return jnp.concatenate([jnp.sin(x), jnp.cos(x), jnp.sin(y), jnp.cos(y)], axis=1)
        patches = _patchify(img, PATCH)
        B, h, w, d = patches.shape
        x = patches.reshape(B, h * w, d)
        x = _layernorm(x, ln1_w)
        x = jnp.einsum('bnd,ed->bne', x, W)
        x = _layernorm(x, ln2_w)
        pe = _posemb_sincos_2d(h, w, x.shape[-1], dtype=x.dtype)
        return x + pe[None, :, :]

    def _L0_attn_ref(x, Wqkv, bqkv, Wo, bo, gamma, beta):
        import jax, jax.numpy as jnp
        import numpy as np
        EPS = 1e-05

        def _apply_rope(t, cos, sin):
            B, H, S, D = t.shape
            tr = t.reshape(B, H, S, D // 2, 2)
            x0, x1 = (tr[..., 0], tr[..., 1])
            r0 = x0 * cos - x1 * sin
            r1 = x0 * sin + x1 * cos
            return jnp.stack([r0, r1], axis=-1).reshape(B, H, S, D)
        B, S, DM = x.shape
        H = 16
        D = DM // H
        qkv = (x @ Wqkv + bqkv).reshape(B, S, 3, H, D)
        qkv = jnp.transpose(qkv, (2, 0, 3, 1, 4))
        q, k, v = (qkv[0], qkv[1], qkv[2])
        inv_freq = 1.0 / 10000.0 ** (jnp.arange(0, D, 2, dtype=jnp.float32) / D)
        pos = jnp.arange(S, dtype=jnp.float32)
        freqs = pos[:, None] * inv_freq[None, :]
        cos, sin = (jnp.cos(freqs), jnp.sin(freqs))
        q = _apply_rope(q, cos, sin)
        k = _apply_rope(k, cos, sin)
        scores = jnp.einsum('bhqd,bhkd->bhqk', q, k) / jnp.sqrt(jnp.float32(D))
        w = jax.nn.softmax(scores, axis=-1)
        attn = jnp.einsum('bhqk,bhkd->bhqd', w, v)
        attn = jnp.transpose(attn, (0, 2, 1, 3)).reshape(B, S, DM)
        out = attn @ Wo + bo
        h = x + out
        mu = jnp.mean(h, axis=-1, keepdims=True)
        var = jnp.mean((h - mu) ** 2, axis=-1, keepdims=True)
        return (h - mu) * jax.lax.rsqrt(var + EPS) * gamma + beta

    def _L0_ffn_ref(x, Wr, W1, W2):
        import math
        import jax, jax.numpy as jnp
        import numpy as np
        B, S, D, F, E = (8, 512, 256, 1024, 8)
        CAPACITY_FACTOR = 1.0
        b, s, d = x.shape
        t = b * s
        cap = max(math.ceil(t * CAPACITY_FACTOR / E), 1)
        xf = x.reshape(t, d)
        probs = jax.nn.softmax(xf.astype(jnp.float32) @ Wr, axis=-1)
        eidx = jnp.argmax(probs, axis=-1)
        p_tok = jnp.take_along_axis(probs, eidx[:, None], axis=1)[:, 0]
        onehot = jax.nn.one_hot(eidx, E, dtype=jnp.int32)
        rank_all = jnp.cumsum(onehot, axis=0) - onehot
        rank = jnp.take_along_axis(rank_all, eidx[:, None], axis=1)[:, 0]
        keep = rank < cap
        slot = jnp.where(keep, rank, cap)
        dispatch = jnp.zeros((E, cap + 1), dtype=jnp.int32).at[eidx, slot].set(jnp.arange(t, dtype=jnp.int32))
        valid = jnp.zeros((E, cap + 1), dtype=bool).at[eidx, slot].set(keep)
        dispatch = dispatch[:, :cap]
        valid = valid[:, :cap]
        xe = xf[dispatch]
        h = jnp.maximum(jnp.einsum('ecd,edf->ecf', xe, W1), 0.0)
        ye = jnp.einsum('ecf,efd->ecd', h, W2)
        pe = p_tok[dispatch]
        ye = ye * (pe * valid.astype(ye.dtype))[:, :, None]
        y = jnp.zeros((t, d), dtype=x.dtype).at[dispatch.reshape(-1)].add(ye.reshape(E * cap, d).astype(x.dtype))
        return y.reshape(b, s, d)
    h = _L0_tok_ref(x, L0_tok_ln1_w, L0_tok_W, L0_tok_ln2_w)
    h = jnp.concatenate([h, txt], axis=1)
    h = h + _L0_attn_ref(_layernorm(h, axis=-1), L0_attn_Wqkv, L0_attn_bqkv, L0_attn_Wo, L0_attn_bo, L0_attn_gamma, L0_attn_beta)
    h = h + _L0_ffn_ref(_layernorm(h, axis=-1), L0_ffn_Wr, L0_ffn_W1, L0_ffn_W2)
    return h

_drawn_inputs = setup_inputs


def setup_inputs(seed=0):
    import zlib

    import numpy as np

    out = dict(_drawn_inputs(seed))
    spreads = {'L0_attn_bqkv': (0.0, 0.447),
     'L0_attn_bo': (0.0, 0.1),
     'L0_attn_gamma': (1.0, 0.2),
     'L0_attn_beta': (0.0, 0.1)}
    factors = {'L0_attn_Wqkv': 3.081}
    for name, (base, spread) in spreads.items():
        noise = np.random.default_rng([zlib.crc32(name.encode()), seed]).standard_normal(out[name].shape)
        drawn = base * np.exp(spread * noise) if base else spread * noise
        out[name] = jnp.asarray(drawn.astype(out[name].dtype))
    for name, factor in factors.items():
        out[name] = (out[name] * factor).astype(out[name].dtype)
    return out
```

```python
import numpy as np
import concourse.bass as bass
import concourse.mybir as mybir
from contextlib import ExitStack

F32 = mybir.dt.float32
BF16 = mybir.dt.bfloat16
U32 = mybir.dt.uint32
ALU = mybir.AluOpType
ACT = mybir.ActivationFunctionType
AX = mybir.AxisListType

P = 128
D = 256
H, DH = 16, 16
HP = 32
NTXT = 77
HW = 14
NIMG = HW * HW
S = NIMG + NTXT
PD = 768
KP = PD // P
NE, FF = 8, 1024
GB = 4
NT = 2 * GB + 1
REM = S - 2 * P
IMG1 = NIMG - P
SB_ = 2 * P + 32
GC = GB * SB_
NQ = H // 4
PARTS = 3
KR = 6 * DH
ROW = D + 4
BIG = 65536.0
EPS = 1e-5
Q_RUNS = ((0, 0, 3), (3, 0, 2), (5, 0, 1))
K_RUNS = ((0, 0, 1), (1, 0, 1), (2, 0, 1), (3, 1, 1), (4, 1, 1), (5, 2, 1))
PRING = 6


def at(g, per, k):
    return g * per + (max(k, 0) + 1)


def settle(eng, sem):
    eng.sem_inc(sem, 1)


class Chain:

    def __init__(self, eng, sem, per):
        self.eng, self.sem, self.per, self.k = eng, sem, per, 0

    def start(self, g):
        self.g, self.k = g, 0

    def link(self, ins):
        ins.then_inc(self.sem, 1)
        self.k += 1
        self.eng.wait_ge(self.sem, at(self.g, self.per, self.k))

    def end(self):
        assert self.k == self.per, (self.k, self.per)


def build_program(nc, nb, chunk, cuts, patches_tok, patches_T, txt, ln1_w, WT, ln2_w, Wqkv, bqkv, Wo, bo,
                  gamma, beta, Wr, W1, W2, pe, rope, masks, tokens, out):
    ng = nb // GB
    ntok = nb * S
    cap = -(-ntok // NE)
    nslot = NE * cap
    out_rows = out.rearrange("b s d -> (b s) d")
    xe = nc.dram_tensor("xe", [nslot, ROW], F32, kind="Internal").ap()
    spread = nc.dram_tensor("spread", [4, PARTS * DH, H // 2, GC], BF16, kind="Internal").ap()

    outer = ExitStack()
    sems = []

    def sem(name):
        s = outer.enter_context(nc.semaphore(name))
        sems.append(s)
        return s

    phase_a(nc, sem, ng, cap, nslot, patches_tok, patches_T, txt, ln1_w, WT, ln2_w, Wqkv, bqkv, Wo, bo,
            gamma, beta, Wr, pe, rope, masks, tokens, out, xe, spread)
    phase_b(nc, sem, cap, ntok, chunk, cuts, xe, W1, W2, out_rows)
    outer.close()


def phase_a(nc, sem, ng, cap, nslot, patches_tok, patches_T, txt, ln1_w, WT, ln2_w, Wqkv, bqkv, Wo, bo,
            gamma, beta, Wr, pe, rope, masks, tokens, out, xe, spread):
    ctx = ExitStack()

    def sb(name, shape, dt=F32):
        return ctx.enter_context(nc.sbuf_tensor(name, shape, dt))

    A_sb = sb("A_sb", [P, KP, D])
    csum = sb("csum", [P, D])
    wqkv = sb("wqkv", [P, 2, 3 * D])
    wo = sb("wo", [P, 2, D])
    wr = sb("wr", [P, 2, NE])
    g1 = sb("g1", [P, KP])
    g2 = sb("g2", [P, D])
    pes = sb("pes", [P, 2, D])
    bq = sb("bq", [P, 3 * D])
    bos = sb("bos", [P, D])
    gam = sb("gam", [P, D])
    bet = sb("bet", [P, D])
    rop = sb("rop", [P, 2, 3, DH // 2])
    msk = sb("msk", [P, 24])
    tokr = sb("tokr", [P, NT])
    idf = sb("idf", [P, P])
    idb = sb("idb", [P, P], BF16)
    onesb = sb("onesb", [P, P], BF16)
    before = sb("before", [P, P], BF16)
    fromb = sb("fromb", [P, GB, P], BF16)
    neghalf = sb("neghalf", [P, NT])
    union = sb("union", [P, 3888])
    pT = union[:, 0:2 * KP * NIMG].rearrange("p (r k n) -> p r k n", r=2, k=KP)
    ptok = union[:, 2 * KP * NIMG:2 * KP * NIMG + 2 * PD].rearrange("p (r n) -> p r n", r=2)
    prob = union[:, 0:PRING * 2 * S].rearrange("p (r c n) -> p r c n", r=PRING, c=2)
    probr = union[:, PRING * 2 * S:(PRING + 1) * 2 * S].rearrange("p (r n) -> p r n", r=2)
    zz = sb("zz", [P, 2, D])
    st = sb("st", [P, 2, 12])
    st2 = sb("st2", [P, 2, 6])
    mv1 = sb("mv1", [P, 2 * GB, 2])
    nm1 = sb("nm1", [P, 2 * GB])
    ve1 = sb("ve1", [P, 2 * GB])
    rs1 = sb("rs1", [P, 2 * GB])
    mv2 = sb("mv2", [P, 2 * GB, 2])
    ve2 = sb("ve2", [P, 2 * GB])
    rp2 = sb("rp2", [P, 2 * GB])
    rs2 = sb("rs2", [P, 2 * GB])
    hN = sb("hN", [P, NT, D])
    stN = sb("stN", [P, NT, 6])
    mvN = sb("mvN", [P, NT, 2])
    veN = sb("veN", [P, NT])
    rsN = sb("rsN", [P, NT])
    hC = sb("hC", [P, NT, D])
    mvC = sb("mvC", [P, NT, 2])
    rsC = sb("rsC", [P, NT])
    xn = sb("xn", [P, 2, D])
    xTs = sb("xTs", [P, 2, D])
    qks = sb("qks", [P, 2, 2 * D])
    rot = sb("rot", [P, 2 * D])
    rest = sb("rest", [P, 4, P])
    ones = rest[:, 0, :]
    comp = sb("comp", [P, PARTS, 4, GC], BF16)
    V = sb("V", [P, NT, H, HP])
    Vbd = sb("Vbd", [P, GB, NQ, P])
    qh = sb("qh", [P, 2, 4, GC], BF16)
    kh = sb("kh", [P, 2, 4, GC], BF16)
    mxs = sb("mxs", [P, 4, NT])
    cs = sb("cs", [P, NT, 4, PARTS], BF16)
    csr = sb("csr", [P, NT, 4])
    O_sb = sb("O_sb", [P, NQ, 2 * GB * P + GB * 32])
    rd = sb("rd", [P, H])
    an = sb("an", [P, H, DH])
    aTs = sb("aTs", [P, D])
    xr = sb("xr", [P, 3, D])
    res = sb("res", [P, 3, D])
    stA = sb("stA", [P, 6])
    mvA = sb("mvA", [P, NT, 2])
    veA = sb("veA", [P, NT])
    rsA = sb("rsA", [P, NT])
    stB = sb("stB", [P, 6])
    mvB = sb("mvB", [P, NT, 2])
    veB = sb("veB", [P, NT])
    y = sb("y", [P, 2, D])
    yTs = sb("yTs", [P, D])
    pay = sb("pay", [P, NT, ROW])
    mx8 = sb("mx8", [P, NT, 8])
    ix8 = sb("ix8", [P, NT, 8], U32)
    lsh = sb("lsh", [P, NT, NE])
    psum_e = sb("psum_e", [P, NT])
    ef = sb("ef", [P, NT])
    oh = sb("oh", [P, NT, NE])
    ohb = sb("ohb", [P, NT, NE], BF16)
    ct = sb("ct", [P, NT, NE])
    ctb = sb("ctb", [P, NT, NE], BF16)
    pairb = sb("pairb", [P, GB, NE], BF16)
    totb = sb("totb", [P, NE], BF16)
    base = sb("base", [P, NE])
    rk = lsh
    rks = sb("rks", [P, NT])
    pen = sb("pen", [P, NT])
    slot = sb("slot", [P, NT])
    slotu = sb("slotu", [P, NT], U32)

    def bank(name, n=1):
        return ctx.enter_context(nc.psum_tensor(name, [P, 512 * n], F32))

    b01, b23, b45, b6, b7 = bank("b01", 2), bank("b23", 2), bank("b45", 2), bank("b6"), bank("b7")
    mxp = b01[:, :].rearrange("p (c n) -> p c n", c=2)
    scp = [b[:, :].rearrange("p (c n) -> p c n", c=2) for b in (b23, b45)]
    z_ps = [b23[:, 0:D], b23[:, 512:512 + D]]
    xT_ps = b01[:, 0:D]
    qk_ps = b01[:, 512:1024]
    v_ps = b23[:, 0:D]
    qkT_ps = b23[:, 512:1024]
    oT_ps = b45[:, 0:512]
    wo_ps = b45[:, 512:512 + D]
    aT_ps, yT_ps = b7[:, 0:D], b7[:, D:2 * D]
    lg_ps = b6[:, 0:NT * NE].rearrange("p (t e) -> p t e", e=NE)
    rk_ps = b6[:, 128:128 + NT * NE]
    tot_ps = b6[:, 256:256 + NE]

    const_in = sem("const_in")
    pool_set = sem("pool_set")
    rows_set = sem("rows_set")
    settled = sem("settled")
    A_ready, csum_ready = sem("A_ready"), sem("csum_ready")
    cs_ps = sem("cs_ps")
    credit = []

    def csem(name, dma=False):
        s = sem(name)
        credit.append((s, dma))
        return s

    ptok_in = [csem(f"ptok_in{i}", 1) for i in range(2)]
    pT_in = [csem(f"pT_in{i}", 1) for i in range(2)]
    txt_in = csem("txt_in", 1)
    ptok_used = csem("ptok_used")
    rs1_in, rs1_ready = csem("rs1_in"), csem("rs1_ready")
    rs2_in, rs2_ready = csem("rs2_in"), csem("rs2_ready")
    z_ready, z_used = csem("z_ready"), csem("z_used")
    zn_ready, emb_ready = csem("zn_ready"), csem("emb_ready")
    rsN_in, rsN_ready = csem("rsN_in"), csem("rsN_ready")
    hN_taken = csem("hN_taken")
    xn_ready, xT_tr, xT_in = csem("xn_ready"), csem("xT_tr"), csem("xT_in")
    qkv_ready, qkv_used = csem("qkv_ready"), csem("qkv_used")
    rope_done, qkT_ready = csem("rope_done"), csem("qkT_ready")
    hi_ready, parts_ready = csem("hi_ready"), csem("parts_ready")
    vbd_ready = csem("vbd_ready")
    spread_out = [csem(f"spread_out{i}", 1) for i in range(2)]
    hat_in = [[csem(f"hat_in{r}{h}", 1) for h in range(2)] for r in range(2)]
    mx_ready, mx_used = csem("mx_ready"), csem("mx_used")
    cs_ready = csem("cs_ready")
    ct_ready = csem("ct_ready")
    cv_done, ca_done = csem("cv_done"), csem("ca_done")
    s_ready, p_ready = csem("s_ready"), csem("p_ready")
    r_ready, pr_ready = csem("r_ready"), csem("pr_ready")
    pv_done, av_ready, o_used = csem("pv_done"), csem("av_ready"), csem("o_used")
    oT_ready, an_ready = csem("oT_ready"), csem("an_ready")
    aT_ready, aT_in = csem("aT_ready"), csem("aT_in")
    xr_ready, xb_ready = csem("xr_ready"), csem("xb_ready")
    wo_ready, wo_used = csem("wo_ready"), csem("wo_used")
    rsA_in, rsA_ready, a_ready = csem("rsA_in"), csem("rsA_ready"), csem("a_ready")
    h2_ready = csem("h2_ready")
    rsB_in, rsB_ready = csem("rsB_in"), csem("rsB_ready")
    y_ready, yT_ready, yT_in, lg_ready = csem("y_ready"), csem("yT_ready"), csem("yT_in"), csem("lg_ready")
    lsh_ready, le_ready = csem("lsh_ready"), csem("le_ready")
    oh_ready, rk_ready, slot_ready = csem("oh_ready"), csem("rk_ready"), csem("slot_ready")
    outw = csem("outw", 1)
    scat = sem("scat")
    scattered = csem("scattered")
    filled = csem("filled", 1)
    v_stepE, v_stepX, v_stepA, v_stepT, v_stepR = (csem("v_step" + c) for c in "EXATR")
    p_stepX, p_stepT, p_stepE = csem("p_stepX"), csem("p_stepT"), csem("p_stepE")

    NFILL = 39
    NHAT = NQ // 2 * (len(Q_RUNS) + len(K_RUNS))
    NCONST = 14
    NWARM = 2
    NMX = NQ * NT
    block = ctx.enter_context(nc.Block())

    def for_dma(g, per, k):
        return at(g, per, k) * 16

    def max_tile(u):
        if u < 8 * GB:
            return u // 2 % 4, 2 * (u // 8) + u % 2
        return u - 8 * GB, 2 * GB

    def max_rows(qd, i):
        src = b01[KR:KR + PARTS, i % 2 * 512:(i % 2 + 1) * 512].bitcast(BF16)
        dst = qh[KR:KR + PARTS, qd % 2, :, :].rearrange("p j (b n) -> p j b n", b=GB)
        if i == 0:
            return dst[:, :, :, 2 * P:SB_], src[:, 0:4 * P].rearrange("p (j b n) -> p j b n", j=4, b=GB)
        return dst[:, i - 1, :, 0:2 * P], src.rearrange("p (b n) -> p b n", b=GB)

    def tile_rows(i):
        return P if i % 2 == 0 else IMG1

    def tile_cols(ap, t):
        if t < 2 * GB:
            c0 = (t // 2) * SB_ + (t % 2) * P
            return ap[:, :, c0:c0 + P]
        return ap.rearrange("p f (b n) -> p f b n", b=GB)[:, :, :, 2 * P:SB_]

    @block.sync
    def _(sp):
        for s, dma in credit:
            sp.sem_inc(s, 16 if dma else 1)
        sp.dma_start(g1[:, :], ln1_w).then_inc(const_in, 16)
        sp.dma_start(A_sb[:, :, :], WT.rearrange("(k p) n -> p k n", p=P)).then_inc(const_in, 16)
        sp.dma_start(wqkv[:, :, :], Wqkv.rearrange("(k p) n -> p k n", p=P)).then_inc(const_in, 16)
        sp.dma_start(wo[:, :, :], Wo.rearrange("(k p) n -> p k n", p=P)).then_inc(const_in, 16)
        sp.dma_start(wr[:, :, :], Wr.rearrange("(k p) n -> p k n", p=P)).then_inc(const_in, 16)
        for dst, src in ((g2, ln2_w), (bq, bqkv), (bos, bo), (gam, gamma), (bet, beta)):
            sp.dma_start(dst[:, :], src.partition_broadcast(P)).then_inc(const_in, 16)
        sp.dma_start(pes[:, :, :], pe).then_inc(const_in, 16)
        sp.dma_start(rop[:, :, :, :], rope).then_inc(const_in, 16)
        sp.dma_start(msk[:, :], masks).then_inc(const_in, 16)
        sp.dma_start(tokr[:, :], tokens).then_inc(const_in, 16)
        sp.wait_ge(pool_set, 1)
        per = nslot // (NFILL * 4)
        assert per * NFILL * 4 == nslot and per <= P
        for i in range(NFILL):
            sp.dma_start(xe[i * per * 4:(i + 1) * per * 4, :].rearrange("(p r) n -> p r n", r=4),
                         pay[0:per, 0:4, :]).then_inc(filled, 16)

        def attn(g, nxt, emb):
            sp.wait_ge(hi_ready, at(g, 9, 9))
            sp.wait_ge(parts_ready, at(g, 9, 9))
            for f in (0, 2, 1, 3):
                sp.dma_start(spread[f].rearrange("(a d) h t -> (d h) a t", a=PARTS), comp[:, :, f, :]
                             ).then_inc(spread_out[f % 2], 16)
            for qd in range(NQ):
                if qd % 2 == 0:
                    sp.wait_ge(spread_out[qd // 2], for_dma(g, 2, 2))
                    settle(sp, settled)
                for hb in range(2):
                    sp.wait_ge(r_ready, at(g, 16, (qd - 2) * GB + 2 * hb + 2))
                    cols = slice(hb * 2 * SB_, (hb + 1) * 2 * SB_)
                    heads = slice(4 * (qd % 2), 4 * (qd % 2) + 4)
                    for dst, f, runs in ((qh, qd // 2, Q_RUNS), (kh, 2 + qd // 2, K_RUNS)):
                        for i, part, n in runs:
                            sp.dma_start(dst[DH * i:DH * (i + n), qd % 2, :, cols],
                                         spread[f, DH * part:DH * (part + n), heads, cols]
                                         ).then_inc(hat_in[qd % 2][hb], 16)
            sp.wait_ge(h2_ready, at(g, 9, 9))
            settle(sp, settled)
            for b in range(GB):
                sp.dma_start(out[bass.ds(g * GB + b, 1), 0:2 * P, :].rearrange("a (c p) d -> p (a c) d", p=P),
                             pay[:, 2 * b:2 * b + 2, 0:D]).then_inc(outw, 16)
                sp.dma_start(out[bass.ds(g * GB + b, 1), 2 * P:S, :].rearrange("a p d -> p (a d)"),
                             pay[32 * b:32 * b + REM, 2 * GB, 0:D]).then_inc(outw, 16)

        with sp.Fori(0, ng) as g:
            attn(g, True, True)
        sp.wait_ge(outw, 16 * at(ng, 8, 0))

    @block.scalar
    def _(act):
        def loads(g):
            if not isinstance(g, int) or g > 1:
                act.wait_ge(av_ready, at(g - 2, 16, 16))
            act.wait_ge(hN_taken, at(g, 1, 0))
            for b in range(GB):
                act.dma_start(hN[IMG1:P, 2 * b + 1, :], txt[bass.ds(g * GB + b, 1), 0:P - IMG1, :]
                              .rearrange("a p d -> p (a d)")).then_inc(txt_in, 16)
                act.dma_start(hN[32 * b:32 * b + REM, 2 * GB, :], txt[bass.ds(g * GB + b, 1), P - IMG1:NTXT, :]
                              .rearrange("a p d -> p (a d)")).then_inc(txt_in, 16)
            for b in range(GB):
                act.wait_ge(z_ready, at(g, 8, 2 * (b - 1) if b >= 2 else 0))
                act.dma_start(pT[:, b % 2, :, :], patches_T[bass.ds(g * GB + b, 1), :, :, :]
                              .rearrange("a p k n -> p (a k) n")).then_inc(pT_in[b % 2], 16)
                for c in range(2):
                    i = 2 * b + c
                    act.wait_ge(ptok_used, at(g, 8, i - 1 if i >= 2 else 0))
                    act.dma_start(ptok[0:tile_rows(i), i % 2, :],
                                  patches_tok[bass.ds(g * GB + b, 1), c * P:c * P + tile_rows(i), :]
                                  .rearrange("a p n -> p (a n)")).then_inc(ptok_in[c], 16)

        def x_tile_a(g, t):
            act.wait_ge(qkv_ready, at(g, 9, t - 1))
            act.wait_ge(xT_tr, at(g, 9, t + 1))
            act.activation(xTs[:, t % 2, :], xT_ps, ACT.Copy).then_inc(xT_in, 1)

        def x_tile_b(g, t):
            if t == 0:
                for place in hat_in[0] + hat_in[1]:
                    act.wait_ge(place, for_dma(g, NHAT, 0))
            act.wait_ge(qkT_ready, at(g, 9, t + 1))
            src = qkT_ps.rearrange("p (f n) -> p f n", f=4)
            if t == 2 * GB:
                src = qkT_ps.rearrange("p (f b n) -> p f b n", f=4, b=GB)
            act.activation(tile_cols(comp[:, 0], t), src, ACT.Copy).then_inc(hi_ready, 1)

        def t_tile_a(g, t):
            act.wait_ge(wo_ready, at(g, 9, t))
            act.wait_ge(aT_ready, at(g, 9, t + 1))
            act.activation(aTs[:, :], aT_ps, ACT.Copy).then_inc(aT_in, 1)

        def t_tile_b(g, t):
            act.wait_ge(lg_ready, at(g, 9, t))
            act.wait_ge(yT_ready, at(g, 9, t + 1))
            act.activation(yTs[:, :], yT_ps, ACT.Copy).then_inc(yT_in, 1)

        def run(g):
            for s in range(NT + 3):
                if 1 <= s < NT + 1:
                    x_tile_a(g, s - 1)
                if 3 <= s < NT + 3:
                    x_tile_b(g, s - 3)

        def c_rows(g, qd, i):
            act.wait_ge(ct_ready, at(g, 5 * NQ, 5 * qd + i + 1))
            dst, src = max_rows(qd, i)
            act.activation(dst, src, ACT.Copy).then_inc(ca_done, 1)

        def o_out(g, qd, b):
            act.wait_ge(av_ready, at(g, 16, qd * GB + b + 1))
            act.activation(O_sb[:, qd, b * 2 * P:(b + 1) * 2 * P], b7[:, 0:2 * P], ACT.Copy)
            act.activation(O_sb[:, qd, 2 * GB * P + 32 * b:2 * GB * P + 32 * b + REM], b7[:, 2 * P:S], ACT.Copy
                           ).then_inc(o_used, 1)

        def attn(g, nxt, emb):
            if nxt:
                act.wait_ge(z_ready, at(g + 1, 8, 8))
                act.wait_ge(ptok_used, at(g + 1, 8, 8))
            act.wait_ge(qkv_used, at(g, 9, 9))
            for b in range(GB):
                for j in range(4):
                    last = act.activation(Vbd[32 * j:32 * j + 32, b, :, 32 * j:32 * j + 32],
                                          V[32 * b:32 * b + 32, 2 * GB, j:H:4, :], ACT.Copy)
            last.then_inc(vbd_ready, 1)
            act.wait_ge(oT_ready, at(g, 9, 0))
            c_rows(g, 0, 2)
            c_rows(g, 0, 4)
            for qd in range(NQ):
                for b in range(GB):
                    for j in range(4):
                        n = (qd * GB + b) * 4 + j
                        act.wait_ge(s_ready, at(g, 64, n + 1))
                        act.wait_ge(pv_done, at(g, 16, (n - PRING) // 4 + 1 if n >= PRING else 0))
                        act.activation(prob[:, n % PRING, :, :], scp[n % 2][:, :, 0:S], ACT.Exp,
                                       scale=float(DH) ** -0.5).then_inc(p_ready, 1)
                        if j == 2 and b >= 1:
                            o_out(g, qd, b - 1)
                    m = qd * GB + b
                    act.wait_ge(r_ready, at(g, 16, m + 1))
                    act.wait_ge(av_ready, at(g, 16, m - 1 if m >= 2 else 0))
                    act.activation(probr[:, m % 2, :], b6[:, 0:S], ACT.Exp,
                                   scale=float(DH) ** -0.5).then_inc(pr_ready, 1)
                if qd + 1 < NQ:
                    c_rows(g, qd + 1, 2)
                o_out(g, qd, GB - 1)
                if qd + 1 < NQ:
                    c_rows(g, qd + 1, 4)
            for s in range(NT + 7):
                if nxt and 1 <= s < NT + 1:
                    x_tile_a(g + 1, s - 1)
                if 1 <= s < NT + 1:
                    t_tile_a(g, s - 1)
                if nxt and 3 <= s < NT + 3:
                    x_tile_b(g + 1, s - 3)
                if 6 <= s < NT + 6:
                    t_tile_b(g, s - 6)
            act.wait_ge(lsh_ready, at(g, 1, 1))
            act.activation(lsh[:, :, :], lsh[:, :, :], ACT.Exp).then_inc(le_ready, 1)
            if emb:
                loads(g + 2)

        act.wait_ge(pool_set, 2)
        loads(0)
        run(0)
        loads(1)
        with act.Fori(0, ng - 2) as g:
            attn(g, True, True)
        attn(ng - 2, True, False)
        attn(ng - 1, False, False)

    @block.gpsimd
    def _(pool):
        pool.memset(pay[:, 0:4, 0:ROW - 1], 0.0)
        pool.memset(pay[:, 0:4, ROW - 1:ROW], BIG).then_inc(pool_set, 1)
        pool.memset(idf[:, :], 0.0)
        pool.memset(idb[:, :], 0.0)
        pool.memset(onesb[:, :], 1.0)
        pool.memset(ones, 1.0)
        pool.memset(before[:, :], 1.0)
        pool.memset(fromb[:, :, :], 1.0)
        pool.memset(neghalf[:, :], -0.5)
        pool.memset(hN[:, :, :], 0.0)
        pool.memset(V[:, :, :, DH + 1:HP], 0.0)
        pool.memset(V[:, :, :, DH:DH + 1], 1.0)
        pool.memset(Vbd[:, :, :, :], 0.0)
        pool.memset(O_sb[:, :, :], 1.0)
        pool.memset(base[:, :], 0.0).then_inc(pool_set, 1)
        pool.wait_ge(pool_set, 2)
        for m in (idf, idb):
            pool.affine_select(out=m[:, :], in_=m[:, :], compare_op=ALU.not_equal, fill=1.0, base=0,
                               pattern=[[-1, P]], channel_multiplier=1)
        pool.affine_select(out=before[:, :], in_=before[:, :], compare_op=ALU.is_gt, fill=0.0, base=0,
                           pattern=[[1, P]], channel_multiplier=-1)
        for b in range(GB):
            last = pool.affine_select(out=fromb[:, b, :], in_=fromb[:, b, :], compare_op=ALU.is_ge, fill=0.0,
                                      base=-32 * b, pattern=[[1, P]], channel_multiplier=0)
        last.then_inc(pool_set, 1)
        pool.wait_ge(const_in, 16 * NCONST)
        pool.wait_ge(pool_set, 3)
        pool.tensor_scalar(V[:, 2 * GB, :, DH], V[:, 2 * GB, :, DH], msk[:, 0:1], 1.0, ALU.mult, ALU.mult
                           ).then_inc(pool_set, 1)

        ex = Chain(pool, p_stepE, 8)
        xx = Chain(pool, p_stepX, 3 * NT)
        tt = Chain(pool, p_stepT, 2 * NT)

        def inv_sqrt(dst, src, n, need, made, value):
            pool.wait_ge(need, value)
            pool.tensor_tensor(dst, src, neghalf[0:dst.shape[0], 0:n], ALU.pow).then_inc(made, 1)

        def e_stage(g):
            ex.start(g)
            for s in range(2 * GB + 2):
                if s < 2 * GB:
                    r = tile_rows(s)
                    inv_sqrt(rs1[0:r, s:s + 1], ve1[0:r, s:s + 1], 1, rs1_in, rs1_ready, at(g, 8, s + 1))
                if 1 <= s < 2 * GB + 1:
                    i = s - 1
                    r = tile_rows(i)
                    inv_sqrt(rp2[0:r, i:i + 1], ve2[0:r, i:i + 1], 1, rs2_in, rs2_ready, at(g, 8, i + 1))
                if s >= 2:
                    i = s - 2
                    r = tile_rows(i)
                    pool.wait_ge(zn_ready, at(g, 8, i + 1))
                    if i == 0:
                        pool.wait_ge(hN_taken, at(g, 1, 0))
                    ex.link(pool.tensor_tensor(zz[0:r, i % 2, :], zz[0:r, i % 2, :], g2[0:r, :], ALU.mult))
                    pool.tensor_tensor(hN[0:r, i, :], zz[0:r, i % 2, :], pes[0:r, i % 2, :], ALU.add
                                       ).then_inc(emb_ready, 1)
            ex.end()
            inv_sqrt(rsN[:, :], veN[:, :], NT, rsN_in, rsN_ready, at(g, 1, 1))

        def rope_tile(g, t):
            pool.wait_ge(qkv_used, at(g, 9, t + 1))
            kind = 2 if t == 2 * GB else t % 2
            x4 = qks[:, t % 2, :].rearrange("p (s a m) -> p s a m", s=4, a=2)
            r4 = rot[:, :].rearrange("p (s a m) -> p s a m", s=4, a=2)
            x3 = qks[:, t % 2, :].rearrange("p (s d h) -> p s d h", s=8, d=DH // 2)

            def table(i, n):
                return rop[:, i, kind, :].unsqueeze(1).unsqueeze(3).broadcast_to([P, n, DH // 2, H // 2])

            def half(ap, a):
                return ap[:, :, a, :].rearrange("p s (d h) -> p s d h", d=DH // 2)

            pool.tensor_tensor(half(r4, 0), half(x4, 1), table(1, 4), ALU.mult)
            xx.link(pool.tensor_tensor(half(r4, 1), half(x4, 0), table(1, 4), ALU.mult))
            xx.link(pool.tensor_tensor(x3, x3, table(0, 8), ALU.mult))
            pool.tensor_tensor(x4[:, :, 0, :], x4[:, :, 0, :], r4[:, :, 0, :], ALU.subtract)
            xx.link(pool.tensor_tensor(x4[:, :, 1, :], x4[:, :, 1, :], r4[:, :, 1, :], ALU.add))
            pool.sem_inc(rope_done, 1)

        def run(g):
            e_stage(g)
            xx.start(g)
            for t in range(NT):
                rope_tile(g, t)
            xx.end()

        def attn(g, nxt, emb):
            if nxt:
                xx.start(g + 1)
            tt.start(g)
            for s in range(NT + 7):
                if nxt and 2 <= s < NT + 2:
                    rope_tile(g + 1, s - 2)
                if 1 <= s < NT + 1:
                    t = s - 1
                    pool.wait_ge(xr_ready, at(g, 9, t + 1))
                    pool.tensor_tensor(xr[:, t % 3, :], xr[:, t % 3, :], bos[:, :], ALU.add).then_inc(xb_ready, 1)
                if 2 <= s < NT + 2:
                    t = s - 2
                    inv_sqrt(rsA[:, t:t + 1], veA[:, t:t + 1], 1, rsA_in, rsA_ready, at(g, 9, t + 1))
                if 3 <= s < NT + 3:
                    t = s - 3
                    pool.wait_ge(a_ready, at(g, 9, t + 1))
                    a = res[:, t % 3, :]
                    tt.link(pool.tensor_tensor(a, a, gam[:, :], ALU.mult))
                    tt.link(pool.tensor_tensor(a, a, bet[:, :], ALU.add))
                    if t == 0:
                        pool.wait_ge(filled, for_dma(0, 0, NFILL))
                        pool.wait_ge(scattered, at(g, 1, 0))
                        pool.wait_ge(outw, for_dma(g, 8, 0))
                    pool.tensor_tensor(pay[:, t, 0:D], a, hC[:, t, :], ALU.add).then_inc(h2_ready, 1)
                if 4 <= s < NT + 4:
                    t = s - 4
                    inv_sqrt(pay[:, t, D + 1:D + 2], veB[:, t:t + 1], 1, rsB_in, rsB_ready, at(g, 9, t + 1))
            if nxt:
                xx.end()
            tt.end()
            if emb:
                e_stage(g + 2)
            pool.wait_ge(slot_ready, at(g, 1, 1))
            settle(pool, settled)
            for t in range(NT):
                pool.indirect_dma_start(out=xe, out_offset=bass.IndirectOffsetOnAxis(ap=slotu[:, t:t + 1], axis=0),
                                        in_=pay[:, t, :], in_offset=None, bounds_check=nslot - 1,
                                        oob_is_err=False).then_inc(scat, 16)
            pool.wait_ge(scat, 16 * NT * (g + 1))
            pool.sem_inc(scattered, 1)

        e_stage(0)
        xx.start(0)
        for t in range(NT):
            rope_tile(0, t)
        xx.end()
        e_stage(1)
        with pool.Fori(0, ng - 2) as g:
            attn(g, True, True)
        attn(ng - 2, True, False)
        attn(ng - 1, False, False)

    @block.vector
    def _(dve):
        ce = Chain(dve, v_stepE, 10 * 8 + 3)
        cx = Chain(dve, v_stepX, 2 * NT + 2)
        ca = Chain(dve, v_stepA, 4 * 4)
        ctn = Chain(dve, v_stepT, 7 * NT)
        cr = Chain(dve, v_stepR, 0)

        dve.memset(qh[KR:P, :, :, :], 0.0)
        dve.memset(kh[KR:P, :, :, :], 0.0).then_inc(rows_set, 1)
        dve.wait_ge(rows_set, 1)
        ones_rows = kh[KR:KR + PARTS, :, :, :].rearrange("p r j (b n) -> p (r j) b n", b=GB)
        dve.memset(ones_rows[:, :, :, 0:S], 1.0)
        dve.wait_ge(const_in, 16 * NCONST)
        for k in range(KP):
            last = dve.tensor_scalar(A_sb[:, k, :], A_sb[:, k, :], g1[:, k:k + 1], None, ALU.mult)
        last.then_inc(A_ready, 1)
        dve.wait_ge(cs_ps, 1)
        dve.tensor_copy(csum[:, :], b6[:, 0:D]).then_inc(csum_ready, 1)
        dve.wait_ge(csum_ready, 1)
        dve.wait_ge(pool_set, 4)

        def e_stage(g):
            ce.start(g)
            for s in range(2 * GB + 2):
                if s < 2 * GB:
                    i, r = s, tile_rows(s)
                    dve.wait_ge(ptok_in[i % 2], for_dma(g, 4, i // 2 + 1))
                    pt = ptok[0:r, i % 2, :].rearrange("p (a n) -> p a n", a=2)
                    dve.bn_stats(st[0:r, i % 2, 0:6], pt[:, 0, :])
                    ce.link(dve.bn_stats(st[0:r, i % 2, 6:12], pt[:, 1, :]))
                    dve.sem_inc(ptok_used, 1)
                    ce.link(dve.bn_aggr(mv1[0:r, i, :], st[0:r, i % 2, :]))
                    dve.tensor_scalar(ve1[0:r, i:i + 1], mv1[0:r, i, 1:2], EPS, None, ALU.add).then_inc(rs1_in, 1)
                    ce.link(dve.tensor_scalar(nm1[0:r, i:i + 1], mv1[0:r, i, 0:1], -1.0, None, ALU.mult))
                if 1 <= s < 2 * GB + 1:
                    i = s - 1
                    r = tile_rows(i)
                    zi = zz[0:r, i % 2, :]
                    dve.wait_ge(emb_ready, at(g, 8, i - 1 if i >= 2 else 0))
                    dve.wait_ge(z_ready, at(g, 8, i + 1))
                    ins = dve.scalar_tensor_tensor(zi, csum[0:r, :], nm1[0:r, i:i + 1], z_ps[i % 2][0:r, :],
                                                   ALU.mult, ALU.add)
                    ce.link(ins)
                    dve.sem_inc(z_used, 1)
                    ce.link(dve.bn_stats(st2[0:r, i % 2, :], zi))
                    settle(dve, settled)
                    ce.link(dve.bn_aggr(mv2[0:r, i, :], st2[0:r, i % 2, :]))
                    dve.wait_ge(rs1_ready, at(g, 8, i + 1))
                    ce.link(dve.tensor_scalar(ve2[0:r, i:i + 1], mv2[0:r, i, 1:2], rs1[0:r, i:i + 1],
                                              rs1[0:r, i:i + 1], ALU.mult, ALU.mult))
                    ce.link(dve.tensor_scalar(ve2[0:r, i:i + 1], ve2[0:r, i:i + 1], EPS, None, ALU.add))
                    dve.sem_inc(rs2_in, 1)
                if s >= 2:
                    i = s - 2
                    r = tile_rows(i)
                    zi = zz[0:r, i % 2, :]
                    dve.wait_ge(rs2_ready, at(g, 8, i + 1))
                    ce.link(dve.tensor_tensor(rs2[0:r, i:i + 1], rp2[0:r, i:i + 1], rs1[0:r, i:i + 1], ALU.mult))
                    ce.link(dve.tensor_scalar(zi, zi, mv2[0:r, i, 0:1], rs2[0:r, i:i + 1], ALU.subtract, ALU.mult))
                    dve.sem_inc(zn_ready, 1)
            dve.wait_ge(emb_ready, at(g, 8, 8))
            dve.wait_ge(txt_in, for_dma(g, 8, 8))
            for t in range(NT):
                last = dve.bn_stats(stN[:, t, :], hN[:, t, :])
            ce.link(last)
            settle(dve, settled)
            for t in range(NT):
                last = dve.bn_aggr(mvN[:, t, :], stN[:, t, :])
            ce.link(last)
            ce.link(dve.tensor_scalar(veN[:, :], mvN[:, :, 1], EPS, None, ALU.add))
            dve.sem_inc(rsN_in, 1)
            ce.end()

        def x_norm(g, t):
            if t == 0:
                dve.wait_ge(rsN_ready, at(g, 1, 1))
            dve.wait_ge(xT_tr, at(g, 9, t - 1))
            dve.tensor_scalar(xn[:, t % 2, :], hN[:, t, :], mvN[:, t, 0:1], rsN[:, t:t + 1],
                              ALU.subtract, ALU.mult).then_inc(xn_ready, 1)

        def x_bias(g, t):
            dve.wait_ge(qkv_ready, at(g, 9, t + 1))
            dve.wait_ge(qkT_ready, at(g, 9, t - 1))
            qk = qks[:, t % 2, :]
            v = V[:, t, :, 0:DH]
            dve.tensor_tensor(qk, qk_ps, bq[:, 0:2 * D], ALU.add)
            ins = dve.tensor_tensor(v, v_ps.rearrange("p (h d) -> p h d", d=DH),
                                    bq[:, 2 * D:3 * D].rearrange("p (h d) -> p h d", d=DH), ALU.add)
            if t == 2 * GB:
                cx.link(ins)
                dve.tensor_scalar(qk, qk, msk[:, 0:1], None, ALU.mult)
                ins = dve.tensor_scalar(v, v, msk[:, 0:1], None, ALU.mult)
            ins.then_inc(qkv_used, 1)

        def x_parts(g, t):
            if t == 0:
                for place in hat_in[0] + hat_in[1]:
                    dve.wait_ge(place, for_dma(g, NHAT, 0))
            dve.wait_ge(hi_ready, at(g, 9, t + 1))
            shape = "p (f b n) -> p f b n" if t == 2 * GB else "p (f n) -> p f n"
            kw = {"f": 4, "b": GB} if t == 2 * GB else {"f": 4}
            r = rest[:, :, :].rearrange("p f n -> p (f n)").rearrange(shape, **kw)
            for f in ([slice(0, 4)] if t < 2 * GB else [slice(i, i + 1) for i in range(4)]):
                last = dve.tensor_tensor(r[:, f], qkT_ps.rearrange(shape, **kw)[:, f],
                                         tile_cols(comp[:, 0], t)[:, f], ALU.subtract)
            cx.link(last)
            for f in ([slice(0, 4)] if t < 2 * GB else [slice(i, i + 1) for i in range(4)]):
                last = dve.tensor_copy(tile_cols(comp[:, 1], t)[:, f], r[:, f])
            cx.link(last)
            for f in ([slice(0, 4)] if t < 2 * GB else [slice(i, i + 1) for i in range(4)]):
                last = dve.tensor_tensor(tile_cols(comp[:, 2], t)[:, f], r[:, f], tile_cols(comp[:, 1], t)[:, f],
                                         ALU.subtract)
            last.then_inc(parts_ready, 1)

        def t_norm(g, t):
            dve.wait_ge(oT_ready, at(g, 9, t + 1))
            o3 = oT_ps.rearrange("p (h d) -> p h d", d=HP)
            ctn.link(dve.reciprocal(rd[:, :], o3[:, :, DH]))
            dve.wait_ge(aT_ready, at(g, 9, t))
            dve.tensor_tensor(an[:, :, :], o3[:, :, 0:DH],
                              rd[:, :].unsqueeze(2).broadcast_to([P, H, DH]), ALU.mult
                              ).then_inc(an_ready, 1)
            dve.tensor_scalar(xr[:, t % 3, :], hC[:, t, :], mvC[:, t, 0:1], rsC[:, t:t + 1],
                              ALU.subtract, ALU.mult).then_inc(xr_ready, 1)

        def t_res(g, t):
            dve.wait_ge(wo_ready, at(g, 9, t + 1))
            dve.wait_ge(xb_ready, at(g, 9, t + 1))
            dve.wait_ge(h2_ready, at(g, 9, t - 2 if t >= 3 else 0))
            r = res[:, t % 3, :]
            ctn.link(dve.tensor_tensor(r, wo_ps, xr[:, t % 3, :], ALU.add))
            dve.sem_inc(wo_used, 1)
            ctn.link(dve.bn_stats(stA[:, :], r))
            settle(dve, settled)
            ctn.link(dve.bn_aggr(mvA[:, t, :], stA[:, :]))
            dve.tensor_scalar(veA[:, t:t + 1], mvA[:, t, 1:2], EPS, None, ALU.add).then_inc(rsA_in, 1)

        def t_apply(g, t):
            dve.wait_ge(rsA_ready, at(g, 9, t + 1))
            r = res[:, t % 3, :]
            dve.tensor_scalar(r, r, mvA[:, t, 0:1], rsA[:, t:t + 1], ALU.subtract, ALU.mult).then_inc(a_ready, 1)

        def t_stats(g, t):
            dve.wait_ge(h2_ready, at(g, 9, t + 1))
            ctn.link(dve.bn_stats(stB[:, :], pay[:, t, 0:D]))
            settle(dve, settled)
            ctn.link(dve.bn_aggr(mvB[:, t, :], stB[:, :]))
            ctn.link(dve.tensor_copy(pay[:, t, D:D + 1], mvB[:, t, 0:1]))
            dve.tensor_scalar(veB[:, t:t + 1], mvB[:, t, 1:2], EPS, None, ALU.add).then_inc(rsB_in, 1)

        def t_y(g, t):
            dve.wait_ge(rsB_ready, at(g, 9, t + 1))
            dve.wait_ge(yT_ready, at(g, 9, t - 1))
            dve.tensor_scalar(y[:, t % 2, :], pay[:, t, 0:D], pay[:, t, D:D + 1], pay[:, t, D + 1:D + 2],
                              ALU.subtract, ALU.mult).then_inc(y_ready, 1)

        def take(g):
            dve.tensor_copy(hC[:, :, :], hN[:, :, :])
            dve.tensor_copy(mvC[:, :, :], mvN[:, :, :])
            cx.link(dve.tensor_copy(rsC[:, :], rsN[:, :]))
            dve.sem_inc(hN_taken, 1)

        def run(g):
            cx.start(g)
            for s in range(NT + 3):
                if s < NT:
                    x_norm(g, s)
                if 2 <= s < NT + 2:
                    x_bias(g, s - 2)
                if 3 <= s < NT + 3:
                    x_parts(g, s - 3)
            take(g)
            cx.end()

        def attn(g, nxt, emb):
            ca.start(g)
            for qd in range(NQ):
                for u in range(NMX):
                    j, t = max_tile(u)
                    dve.wait_ge(mx_ready, at(g, NQ * NMX, qd * NMX + u + 1))
                    dve.tensor_reduce(mxs[:, j, t:t + 1], mxp[:, u % 2, 0:S], AX.X, ALU.max).then_inc(mx_used, 1)
                dve.wait_ge(mx_used, at(g, NQ * NMX, (qd + 1) * NMX))
                dve.wait_ge(ct_ready, at(g, 5 * NQ, 5 * qd))
                mt = mxs[:, :, :].rearrange("p j t -> p t j")
                ca.link(dve.tensor_scalar(cs[:, :, :, 0], mt, -1.0, None, ALU.mult))
                ca.link(dve.scalar_tensor_tensor(csr[:, :, :], mt, -1.0, cs[:, :, :, 0], ALU.mult, ALU.subtract))
                ca.link(dve.tensor_copy(cs[:, :, :, 1], csr[:, :, :]))
                ca.link(dve.tensor_tensor(cs[:, :, :, 2], csr[:, :, :], cs[:, :, :, 1], ALU.subtract))
                dve.sem_inc(cs_ready, 1)
                for i in (0, 1, 3):
                    dve.wait_ge(ct_ready, at(g, 5 * NQ, 5 * qd + i + 1))
                    dst, src = max_rows(qd, i)
                    if i:
                        dve.tensor_copy(dst, src).then_inc(cv_done, 1)
                    else:
                        for j in range(4):
                            last = dve.tensor_copy(dst[:, j], src[:, j])
                        last.then_inc(cv_done, 1)
            ca.end()
            ctn.start(g)
            if nxt:
                cx.start(g + 1)
            for s in range(NT + 7):
                if nxt and s < NT:
                    x_norm(g + 1, s)
                if s < NT:
                    t_norm(g, s)
                if nxt and 2 <= s < NT + 2:
                    if s == 2:
                        dve.wait_ge(av_ready, at(g, 16, 16))
                        dve.wait_ge(vbd_ready, at(g, 1, 1))
                    x_bias(g + 1, s - 2)
                if 2 <= s < NT + 2:
                    t_res(g, s - 2)
                if nxt and 3 <= s < NT + 3:
                    x_parts(g + 1, s - 3)
                if 3 <= s < NT + 3:
                    t_apply(g, s - 3)
                if 4 <= s < NT + 4:
                    t_stats(g, s - 4)
                if 5 <= s < NT + 5:
                    t_y(g, s - 5)
            if nxt:
                dve.wait_ge(h2_ready, at(g, 9, 9))
                take(g + 1)
                cx.end()
            ctn.end()
            route_1(g)
            if emb:
                e_stage(g + 2)
            route_2(g)

        def route_1(g):
            cr.start(g)
            dve.wait_ge(lg_ready, at(g, 9, 9))
            settle(dve, settled)
            for t in range(NT):
                last = dve.max(mx8[:, t, :], lg_ps[:, t, :])
            cr.link(last)
            settle(dve, settled)
            for t in range(NT):
                last = dve.max_index(ix8[:, t, :], mx8[:, t, :], lg_ps[:, t, :])
            cr.link(last)
            dve.tensor_tensor(lsh[:, :, :], lg_ps, mx8[:, :, 0:1].broadcast_to([P, NT, NE]), ALU.subtract
                              ).then_inc(lsh_ready, 1)
            cr.link(dve.tensor_copy(ef[:, :], ix8[:, :, 0]))
            iota = msk[:, 8:16].unsqueeze(1).broadcast_to([P, NT, NE])
            cr.link(dve.tensor_tensor(oh[:, :, :], iota, ef[:, :].unsqueeze(2).broadcast_to([P, NT, NE]),
                                      ALU.is_equal))
            cr.link(dve.tensor_scalar(oh[:, 2 * GB, :], oh[:, 2 * GB, :], msk[:, 0:1], None, ALU.mult))
            dve.tensor_copy(ohb[:, :, :], oh[:, :, :])
            cr.link(dve.memset(ct[:, 0, :], 0.0))
            for t in range(1, 2 * GB):
                cr.link(dve.tensor_tensor(ct[:, t, :], ct[:, t - 1, :], oh[:, t - 1, :], ALU.add))
            cr.link(dve.memset(ct[:, 2 * GB, :], 0.0))
            for b in range(1, GB):
                last = dve.scalar_tensor_tensor(
                    ct[:, 2 * b:2 * b + 2, :],
                    oh[:, 2 * GB, :].unsqueeze(1).broadcast_to([P, 2, NE]),
                    msk[:, b:b + 1], ct[:, 2 * b:2 * b + 2, :], ALU.mult, ALU.add)
            cr.link(last)
            pr = oh[:, 0:2 * GB, :].rearrange("p (b c) e -> p b c e", c=2)
            dve.tensor_tensor(pairb[:, :, :], pr[:, :, 0, :], pr[:, :, 1, :], ALU.add)
            with nc.allow_low_precision(reason="counts up to 9 are exact in bfloat16"):
                dve.tensor_reduce(totb[:, :], oh[:, :, :].rearrange("p t e -> p e t"), AX.X, ALU.add)
            dve.tensor_copy(ctb[:, :, :], ct[:, :, :]).then_inc(oh_ready, 1)
            dve.wait_ge(le_ready, at(g, 1, 1))
            cr.link(dve.tensor_reduce(psum_e[:, :], lsh[:, :, :], AX.X, ALU.add))
            cr.link(dve.reciprocal(pay[:, :, D + 2], psum_e[:, :]))

        def route_2(g):
            dve.wait_ge(rk_ready, at(g, 1, 1))
            cr.link(dve.tensor_tensor(rk[:, :, :], rk_ps.rearrange("p (t e) -> p t e", e=NE),
                                      base[:, :].unsqueeze(1).broadcast_to([P, NT, NE]), ALU.add))
            cr.link(dve.tensor_tensor(rk[:, :, :], rk[:, :, :], oh[:, :, :], ALU.mult))
            cr.link(dve.tensor_reduce(rks[:, :], rk[:, :, :], AX.X, ALU.add))
            dve.tensor_tensor(base[:, :], base[:, :], tot_ps, ALU.add)
            dve.tensor_scalar(pen[:, :], rks[:, :], float(cap), BIG, ALU.is_ge, ALU.mult)
            cr.link(dve.scalar_tensor_tensor(slot[:, :], ef[:, :], float(cap), rks[:, :], ALU.mult, ALU.add))
            cr.link(dve.tensor_tensor(slot[:, :], slot[:, :], pen[:, :], ALU.add))
            cr.link(dve.tensor_scalar(slot[:, 2 * GB:NT], slot[:, 2 * GB:NT], msk[:, 4:5], None, ALU.add))
            dve.wait_ge(scattered, at(g, 1, 0))
            cr.link(dve.tensor_copy(slotu[:, :], slot[:, :]))
            cr.link(dve.tensor_copy(pay[:, :, D + 3], tokr[:, :]))
            cr.link(dve.tensor_scalar(tokr[:, :], tokr[:, :], float(GB * S), None, ALU.add))
            dve.sem_inc(slot_ready, 1)
            cr.end()

        cr.per = 26
        e_stage(0)
        run(0)
        e_stage(1)
        with dve.Fori(0, ng - 2) as g:
            attn(g, True, True)
        attn(ng - 2, True, False)
        attn(ng - 1, False, False)

    @block.tensor
    def _(pe_):
        mm = pe_.matmul
        pe_.wait_ge(A_ready, 1)
        pe_.wait_ge(pool_set, 4)
        for k in range(KP):
            last = mm(b6[:, 0:D], ones, A_sb[:, k, :], start=(k == 0), stop=(k == KP - 1))
        last.then_inc(cs_ps, 1)
        pe_.wait_ge(csum_ready, 1)

        def e_stage(g):
            pe_.wait_ge(qkv_used, at(g, 9, 0))
            pe_.wait_ge(parts_ready, at(g, 9, 0))
            for i in range(2 * GB):
                b, c, r = i // 2, i % 2, tile_rows(i)
                pe_.wait_ge(pT_in[b % 2], for_dma(g, 2, b // 2 + 1))
                pe_.wait_ge(z_used, at(g, 8, i - 1))
                for k in range(KP):
                    last = mm(z_ps[i % 2][0:r, :], pT[:, b % 2, k, c * P:c * P + r], A_sb[:, k, :],
                              start=(k == 0), stop=(k == KP - 1))
                last.then_inc(z_ready, 1)

        def x_transpose(g, t):
            pe_.wait_ge(xn_ready, at(g, 9, t + 1))
            pe_.wait_ge(xT_in, at(g, 9, t))
            for k in range(2):
                last = pe_.transpose(xT_ps[:, k * P:(k + 1) * P], xn[:, t % 2, k * P:(k + 1) * P], idf[:, :])
            last.then_inc(xT_tr, 1)

        def x_project(g, t):
            pe_.wait_ge(xT_in, at(g, 9, t + 1))
            pe_.wait_ge(qkv_used, at(g, 9, t))
            for k in range(2):
                mm(qk_ps, xTs[:, t % 2, k * P:(k + 1) * P], wqkv[:, k, 0:2 * D], start=(k == 0), stop=(k == 1))
            for k in range(2):
                last = mm(v_ps, xTs[:, t % 2, k * P:(k + 1) * P], wqkv[:, k, 2 * D:3 * D],
                          start=(k == 0), stop=(k == 1))
            last.then_inc(qkv_ready, 1)

        def x_turn(g, t):
            pe_.wait_ge(rope_done, at(g, 9, t + 1))
            pe_.wait_ge(parts_ready, at(g, 9, t))
            for f in range(4):
                last = pe_.transpose(qkT_ps[:, f * P:(f + 1) * P], qks[:, t % 2, f * P:(f + 1) * P], idf[:, :])
            last.then_inc(qkT_ready, 1)

        def run(g):
            for s in range(NT + 3):
                if 1 <= s < NT + 1:
                    x_transpose(g, s - 1)
                if 3 <= s < NT + 3:
                    x_turn(g, s - 3)
                if 1 <= s < NT + 1:
                    x_project(g, s - 1)

        def max_unit(g, qd, u):
            pe_.wait_ge(mx_used, at(g, NQ * NMX, qd * NMX + u - 1))
            q, k = qh[0:KR, qd % 2], kh[0:KR, qd % 2]
            j, t = max_tile(u)
            if t < 2 * GB:
                b = t // 2
                if u % 16 == 0:
                    pe_.wait_ge(hat_in[qd % 2][b // 2], for_dma(g, NHAT, (qd // 2 + 1) * (NHAT // 2)))
                if u == 0:
                    pe_.wait_ge(cv_done, at(g, 3 * NQ, 3 * qd))
                    pe_.wait_ge(ca_done, at(g, 2 * NQ, 2 * qd))
                last = mm(mxp[:, u % 2, 0:S], q[:, j, b * SB_ + t % 2 * P:b * SB_ + (t % 2 + 1) * P],
                          k[:, j, b * SB_:b * SB_ + S], start=True, stop=True)
            else:
                for b in range(GB):
                    last = mm(mxp[32 * b:32 * b + 32, u % 2, 0:S], q[:, j, b * SB_ + 2 * P:(b + 1) * SB_],
                              k[:, j, b * SB_:b * SB_ + S], start=True, stop=True)
            last.then_inc(mx_ready, 1)

        def max_turn(g, qd, i):
            if i == 0:
                pe_.wait_ge(cs_ready, at(g, NQ, qd + 1))
            elif i == 4:
                pe_.wait_ge(ca_done, at(g, 2 * NQ, 2 * qd + 1))
            elif i > 1:
                pe_.wait_ge(cv_done, at(g, 3 * NQ, 3 * qd + i - 1))
            dst = b01[KR:KR + PARTS, i % 2 * 512:(i % 2 + 1) * 512].bitcast(BF16)
            for k in range(4 if i == 0 else 2 * GB):
                last = pe_.transpose(dst[:, k * P:(k + 1) * P], cs[:, 2 * GB, k, :] if i == 0 else cs[:, k, i - 1, :],
                                     idb[:, :])
            last.then_inc(ct_ready, 1)

        def score_unit(g, qd, b, j):
            n = (qd * GB + b) * 4 + j
            pe_.wait_ge(p_ready, at(g, 64, n - 1))
            if b == 0:
                if j % 2 == 0:
                    pe_.wait_ge(cv_done, at(g, 3 * NQ, 3 * qd + 2 + j // 2))
                else:
                    pe_.wait_ge(ca_done, at(g, 2 * NQ, 2 * qd + 1 + j // 2))
            q, k = qh[:, qd % 2, j], kh[:, qd % 2, j]
            for c in range(2):
                last = mm(scp[n % 2][:, c, 0:S], k[:, b * SB_ + c * P:b * SB_ + (c + 1) * P],
                          q[:, b * SB_:b * SB_ + S], start=True, stop=True)
            last.then_inc(s_ready, 1)

        def score_rem(g, qd, b):
            m = qd * GB + b
            pe_.wait_ge(pr_ready, at(g, 16, m))
            for j in range(4):
                last = mm(b6[32 * j:32 * j + 32, 0:S], kh[:, qd % 2, j, b * SB_ + 2 * P:(b + 1) * SB_],
                          qh[:, qd % 2, j, b * SB_:b * SB_ + S], start=True, stop=True)
            last.then_inc(r_ready, 1)

        def value_unit(g, qd, b, c):
            m = qd * GB + b
            if c == 0:
                pe_.wait_ge(p_ready, at(g, 64, 4 * m + 4))
                pe_.wait_ge(o_used, at(g, 16, m))
            if c < 2:
                for j in range(4):
                    n = 4 * m + j
                    last = mm(b7[32 * j:32 * j + 32, 0:S], V[:, 2 * b + c, 4 * qd + j, :], prob[:, n % PRING, c, :],
                              start=(c == 0), stop=False, skip_group_check=True)
                if c == 1:
                    last.then_inc(pv_done, 1)
            else:
                pe_.wait_ge(pr_ready, at(g, 16, m + 1))
                mm(b7[:, 0:S], Vbd[:, b, qd, :], probr[:, m % 2, :], start=False, stop=True, skip_group_check=True
                   ).then_inc(av_ready, 1)

        def attn(g, nxt, emb):
            pe_.wait_ge(slot_ready, at(g, 1, 0))
            pe_.wait_ge(vbd_ready, at(g, 1, 1))
            for s_ in (qkv_used, xT_in, parts_ready):
                pe_.wait_ge(s_, at(g, 9, 9))
            for s_ in (aT_in, wo_used, yT_in, an_ready):
                pe_.wait_ge(s_, at(g, 9, 0))
            pe_.wait_ge(z_used, at(g + 1, 8, 8) if emb or nxt else at(g + 1, 8, 0))
            for u in range(NMX):
                max_unit(g, 0, u)
            for i in range(5):
                max_turn(g, 0, i)
            for qd in range(NQ):
                pe_.wait_ge(p_ready, at(g, 64, 16 * qd - 1))
                for _ in range(NWARM):
                    mm(scp[0][:, 0, :], idf[:, :], wqkv[:, 0, 0:512], start=True, stop=True)
                for b in range(GB):
                    for j in range(4):
                        score_unit(g, qd, b, j)
                        if qd + 1 < NQ and b < GB - 1:
                            for i in range(NMX // (4 * (GB - 1))):
                                max_unit(g, qd + 1, (4 * b + j) * (NMX // (4 * (GB - 1))) + i)
                        if b >= 1 and j < 3:
                            value_unit(g, qd, b - 1, j)
                    if qd + 1 < NQ and b == GB - 1:
                        max_turn(g, qd + 1, 0)
                        max_turn(g, qd + 1, 1)
                    score_rem(g, qd, b)
                for c in range(3):
                    value_unit(g, qd, GB - 1, c)
                    if qd + 1 < NQ:
                        max_turn(g, qd + 1, 2 + c)
            pe_.wait_ge(cv_done, at(g, 3 * NQ, 3 * NQ))
            pe_.wait_ge(ca_done, at(g, 2 * NQ, 2 * NQ))
            pe_.wait_ge(p_ready, at(g, 64, 64))
            pe_.wait_ge(pr_ready, at(g, 16, 16))
            for s in range(NT + 7):
                if nxt and 1 <= s < NT + 1:
                    x_transpose(g + 1, s - 1)
                if s < NT:
                    t = s
                    if t == 0:
                        pe_.wait_ge(o_used, at(g, 16, 16))
                    pe_.wait_ge(an_ready, at(g, 9, t))
                    for qd in range(NQ):
                        last = pe_.transpose(oT_ps[:, qd * P:(qd + 1) * P], O_sb[:, qd, t * P:(t + 1) * P], idf[:, :])
                    last.then_inc(oT_ready, 1)
                if 1 <= s < NT + 1:
                    t = s - 1
                    pe_.wait_ge(an_ready, at(g, 9, t + 1))
                    pe_.wait_ge(aT_in, at(g, 9, t))
                    pe_.wait_ge(yT_in, at(g, 9, t - 5))
                    for k in range(2):
                        last = pe_.transpose(aT_ps[:, k * P:(k + 1) * P],
                                             an[:, 8 * k:8 * k + 8, :].rearrange("p h d -> p (h d)"), idf[:, :])
                    last.then_inc(aT_ready, 1)
                if 6 <= s < NT + 6:
                    t = s - 6
                    pe_.wait_ge(y_ready, at(g, 9, t + 1))
                    pe_.wait_ge(yT_in, at(g, 9, t))
                    pe_.wait_ge(aT_in, at(g, 9, min(t + 6, NT)))
                    for k in range(2):
                        last = pe_.transpose(yT_ps[:, k * P:(k + 1) * P], y[:, t % 2, k * P:(k + 1) * P], idf[:, :])
                    last.then_inc(yT_ready, 1)
                if nxt and 3 <= s < NT + 3:
                    x_turn(g + 1, s - 3)
                if nxt and 1 <= s < NT + 1:
                    x_project(g + 1, s - 1)
                if 1 <= s < NT + 1:
                    t = s - 1
                    pe_.wait_ge(aT_in, at(g, 9, t + 1))
                    pe_.wait_ge(wo_used, at(g, 9, t))
                    for k in range(2):
                        last = mm(wo_ps, aTs[:, k * P:(k + 1) * P], wo[:, k, :], start=(k == 0), stop=(k == 1))
                    last.then_inc(wo_ready, 1)
                if 6 <= s < NT + 6:
                    t = s - 6
                    pe_.wait_ge(yT_in, at(g, 9, t + 1))
                    for k in range(2):
                        last = mm(lg_ps[:, t, :], yTs[:, k * P:(k + 1) * P], wr[:, k, :], start=(k == 0), stop=(k == 1))
                    last.then_inc(lg_ready, 1)
            if emb:
                e_stage(g + 2)
            pe_.wait_ge(oh_ready, at(g, 1, 1))
            mm(rk_ps, before[:, :], ohb[:, :, :].rearrange("p t e -> p (t e)"), start=True, stop=False,
               skip_group_check=True)
            mm(rk_ps, onesb[:, :], ctb[:, :, :].rearrange("p t e -> p (t e)"), start=False, stop=False,
               skip_group_check=True)
            for b in range(GB):
                mm(rk_ps[:, 2 * GB * NE:NT * NE], fromb[:, b, :], pairb[:, b, :], start=False, stop=(b == GB - 1),
                   skip_group_check=True)
            mm(tot_ps, onesb[:, :], totb[:, :], start=True, stop=True).then_inc(rk_ready, 1)

        e_stage(0)
        run(0)
        e_stage(1)
        with pe_.Fori(0, ng - 2) as g:
            attn(g, True, True)
        attn(ng - 2, True, False)
        attn(ng - 1, False, False)

    ctx.close()


def phase_b(nc, sem, cap, ntok, chunk, cuts, xe, W1, W2, out_rows):
    ctx = ExitStack()

    def sb(name, shape, dt=F32):
        return ctx.enter_context(nc.sbuf_tensor(name, shape, dt))

    nch = cap // chunk
    UN = 2 * nch
    RB = 3 if UN % 3 == 0 else 2
    KF = FF // P
    NC = len(cuts)
    offs = [sum(cuts[:i]) for i in range(NC)]
    w1 = sb("w1", [P, 2, 2, FF])
    w2 = sb("w2", [P, 2, KF, D])
    rows = sb("rows", [P, RB, NC, ROW])
    yb = sb("yb", [P, 2, NC, D])
    yT = sb("yT", [P, 2, 2, chunk])
    hT = sb("hT", [P, 2, KF, chunk])
    ob = sb("ob", [P, RB, NC, D])
    idx = sb("idx", [P, RB, NC], U32)
    idf = sb("idf2", [P, P])

    def bank(name):
        return ctx.enter_context(nc.psum_tensor(name, [P, 512], F32))

    yT_ps = [bank(f"yTp{k}") for k in range(2)]
    h_ps = [bank(f"hp{k}") for k in range(4)]
    o_ps = [bank(f"op{k}") for k in range(2)]

    credit = []

    def csem(name, dma=False):
        s = sem(name)
        credit.append((s, dma))
        return s

    w_in = [csem(f"w_in{i}", 1) for i in range(2)]
    rows_in = [csem(f"rows_in{i}", 1) for i in range(RB)]
    ow = sem("ow")
    scattered = csem("out_scattered")
    id_ready, id_zero, settled = sem("id_ready"), sem("id_zero"), sem("out_settled")
    yb_ready, yT_tr, yT_sb = csem("yb_ready"), csem("yT_tr"), csem("yT_sb")
    h_ready = csem("h_ready")
    hA, hV = csem("hA"), csem("hV")
    o_ready, ob_ready = csem("o_ready"), csem("ob_ready")
    block = ctx.enter_context(nc.Block())

    @block.sync
    def _(sp):
        for s, dma in credit:
            sp.sem_inc(s, 16 if dma else 1)
        def weights(expert, buf):
            sp.dma_start(w1[:, buf, :, :], W1[bass.ds(expert, 1), :, :].rearrange("a (k p) n -> p (a k) n", p=P)
                         ).then_inc(w_in[buf], 16)
            sp.dma_start(w2[:, buf, :, :], W2[bass.ds(expert, 1), :, :].rearrange("a (k p) n -> p (a k) n", p=P)
                         ).then_inc(w_in[buf], 16)

        def pair(e2, last):
            for c in range(UN):
                sp.wait_ge(ob_ready, at(e2, UN * NC, (c - RB + 1) * NC if c >= RB else 0))
                settle(sp, settled)
                for i in range(NC):
                    sp.dma_start(rows[0:cuts[i], c % RB, i, :],
                                 xe[bass.ds(e2 * (2 * cap) + (c * chunk + offs[i]), cuts[i]), :]).then_inc(rows_in[c % RB], 16)
                if c == 0:
                    weights(e2 * 2 + 1, 1)
                if c == nch and not last:
                    sp.wait_ge(o_ready, at(e2, UN * NC, nch * NC))
                    settle(sp, settled)
                    weights(e2 * 2 + 2, 0)

        weights(0, 0)
        with sp.Fori(0, NE // 2 - 1) as e2:
            pair(e2, False)
        pair(NE // 2 - 1, True)

    @block.gpsimd
    def _(pool):
        pool.memset(idf[:, :], 0.0).then_inc(id_zero, 1)
        pool.wait_ge(id_zero, 1)
        pool.affine_select(out=idf[:, :], in_=idf[:, :], compare_op=ALU.not_equal, fill=1.0, base=0,
                           pattern=[[-1, P]], channel_multiplier=1).then_inc(id_ready, 1)
        with pool.Fori(0, NE // 2) as e2:
            for c in range(UN):
                pool.wait_ge(ob_ready, at(e2, UN * NC, (c + 1) * NC))
                settle(pool, settled)
                for i in range(NC):
                    pool.indirect_dma_start(
                        out=out_rows, out_offset=bass.IndirectOffsetOnAxis(ap=idx[0:cuts[i], c % RB, i:i + 1], axis=0),
                        in_=ob[0:cuts[i], c % RB, i, :], in_offset=None, bounds_check=ntok - 1,
                        oob_is_err=False).then_inc(ow, 16)
                pool.wait_ge(ow, 16 * NC * (e2 * UN + (c + 1)))
                pool.sem_inc(scattered, 1)

    @block.vector
    def _(dve):
        def norm(e2, c):
            dve.wait_ge(rows_in[c % RB], 16 * at(e2, UN * NC // RB, (c // RB + 1) * NC))
            dve.wait_ge(yT_tr, at(e2, UN, c - 1))
            for i in range(NC):
                n = cuts[i]
                r = rows[0:n, c % RB, i, :]
                last = dve.tensor_scalar(yb[0:n, c % 2, i, :], r[:, 0:D], r[:, D:D + 1], r[:, D + 1:D + 2],
                                         ALU.subtract, ALU.mult)
            last.then_inc(yb_ready, 1)

        def relu(e2, c, f):
            dve.wait_ge(h_ready, at(e2, UN * KF, c * KF + f + 1))
            if f == 1:
                dve.wait_ge(o_ready, at(e2, UN * NC, (c - 1) * NC if c >= 2 else 0))
            dve.tensor_scalar(hT[:, c % 2, f, :], h_ps[f % 4][:, 0:chunk], 0.0, None, ALU.max).then_inc(hV, 1)

        def result(e2, c, i):
            n = cuts[i]
            r = rows[0:n, c % RB, i, :]
            if i == 0:
                dve.wait_ge(scattered, at(e2, UN, c - RB + 1 if c >= RB else 0))
            dve.wait_ge(o_ready, at(e2, UN * NC, c * NC + i + 1))
            dve.tensor_copy(idx[0:n, c % RB, i:i + 1], r[:, D + 3:D + 4])
            dve.scalar_tensor_tensor(ob[0:n, c % RB, i, :], o_ps[i % 2][0:n, 0:D], r[:, D + 2:D + 3], r[:, 0:D],
                                     ALU.mult, ALU.add).then_inc(ob_ready, 1)

        with dve.Fori(0, NE // 2) as e2:
            norm(e2, 0)
            for c in range(UN):
                if c + 1 < UN:
                    norm(e2, c + 1)
                for f in range(1, KF, 2):
                    relu(e2, c, f)
                for i in range(NC):
                    result(e2, c, i)

    @block.scalar
    def _(act):
        def turn(e2, c):
            act.wait_ge(yT_tr, at(e2, UN, c + 1))
            act.wait_ge(h_ready, at(e2, UN * KF, (c - 1) * KF if c >= 2 else 0))
            act.activation(yT[:, c % 2, 0, :], yT_ps[0][:, 0:chunk], ACT.Copy)
            act.activation(yT[:, c % 2, 1, :], yT_ps[1][:, 0:chunk], ACT.Copy).then_inc(yT_sb, 1)

        with act.Fori(0, NE // 2) as e2:
            turn(e2, 0)
            for c in range(UN):
                for f in range(0, KF, 2):
                    act.wait_ge(h_ready, at(e2, UN * KF, c * KF + f + 1))
                    if f == 0:
                        act.wait_ge(o_ready, at(e2, UN * NC, (c - 1) * NC if c >= 2 else 0))
                    act.activation(hT[:, c % 2, f, :], h_ps[f % 4][:, 0:chunk], ACT.Relu).then_inc(hA, 1)
                    if f == 2 and c + 1 < UN:
                        turn(e2, c + 1)

    @block.tensor
    def _(pe_):
        mm = pe_.matmul
        pe_.wait_ge(id_ready, 1)

        def turn(e2, c):
            pe_.wait_ge(yb_ready, at(e2, UN, c + 1))
            pe_.wait_ge(yT_sb, at(e2, UN, c))
            for i in range(NC):
                n = cuts[i]
                for k in range(2):
                    last = pe_.transpose(yT_ps[k][:, offs[i]:offs[i] + n], yb[0:n, c % 2, i, k * P:(k + 1) * P],
                                         idf[0:n, 0:n])
            last.then_inc(yT_tr, 1)

        with pe_.Fori(0, NE // 2) as e2:
            turn(e2, 0)
            for c in range(UN):
                e = c // nch
                if c % nch == 0:
                    pe_.wait_ge(w_in[e], 16 * at(e2, 2, 2))
                pe_.wait_ge(yT_sb, at(e2, UN, c + 1))
                for f in range(KF):
                    n = c * KF + f - 4
                    pe_.wait_ge(hA if f % 2 == 0 else hV, at(e2, UN * KF // 2, n // 2 + 1))
                    for k in range(2):
                        last = mm(h_ps[f % 4][:, 0:chunk], w1[:, e, k, f * P:(f + 1) * P], yT[:, c % 2, k, :],
                                  start=(k == 0), stop=(k == 1))
                    last.then_inc(h_ready, 1)
                    if f == 1 and c + 1 < UN:
                        turn(e2, c + 1)
                for i in range(NC):
                    m = c * NC + i
                    pe_.wait_ge(ob_ready, at(e2, UN * NC, m - 1))
                    for f in range(KF):
                        if i == 0:
                            pe_.wait_ge(hA if f % 2 == 0 else hV, at(e2, UN * KF // 2, (c * KF + f) // 2 + 1))
                        last = mm(o_ps[i % 2][0:cuts[i], 0:D], hT[:, c % 2, f, offs[i]:offs[i] + cuts[i]],
                                  w2[:, e, f, :], start=(f == 0), stop=(f == KF - 1))
                    last.then_inc(o_ready, 1)

    ctx.close()


def host_constants():
    dim4 = D // 4
    yy, xx = np.meshgrid(np.arange(HW, dtype=np.float32), np.arange(HW, dtype=np.float32), indexing="ij")
    omega = (1.0 / (np.float32(10000.0) ** (np.arange(dim4, dtype=np.float32) / (dim4 - 1)))).astype(np.float32)
    ya, xa = yy.reshape(-1)[:, None] * omega[None, :], xx.reshape(-1)[:, None] * omega[None, :]
    pos = np.concatenate([np.sin(xa), np.cos(xa), np.sin(ya), np.cos(ya)], axis=1).astype(np.float32)
    pe = np.zeros((P, 2, D), np.float32)
    pe[:, 0] = pos[:P]
    pe[:IMG1, 1] = pos[P:]
    inv = (1.0 / np.float32(10000.0) ** (np.arange(0, DH, 2, dtype=np.float32) / DH)).astype(np.float32)
    where = np.stack([np.arange(P), P + np.arange(P), 2 * P + np.arange(P) % 32]).astype(np.float32)
    ang = (where[:, :, None] * inv).astype(np.float32)
    rope = np.stack([np.cos(ang), np.sin(ang)]).astype(np.float32)
    rope = np.ascontiguousarray(rope.transpose(2, 0, 1, 3))
    row = np.arange(P)
    valid = (row % 32 < REM).astype(np.float32)
    masks = np.zeros((P, 24), np.float32)
    masks[:, 0] = valid
    for b in range(1, GB):
        masks[:, b] = valid * (row < 32 * b)
    masks[:, 4] = (1 - valid) * BIG
    masks[:, 8:16] = np.arange(NE)
    tokens = np.zeros((P, NT), np.float32)
    for t in range(2 * GB):
        tokens[:, t] = (t // 2) * S + (t % 2) * P + row
    tokens[:, 2 * GB] = (row // 32) * S + 2 * P + row % 32
    return pe, rope, masks, tokens


_ORDER = ["patches_tok", "patches_T", "txt", "ln1_w", "WT", "ln2_w", "Wqkv", "bqkv", "Wo", "bo",
          "gamma", "beta", "Wr", "W1", "W2", "pe", "rope", "masks", "tokens"]


def lay_out(i):
    x = np.asarray(i["x"])
    nb = x.shape[0]
    p = x.reshape(nb, 3, HW, 16, HW, 16).transpose(0, 2, 4, 1, 3, 5).reshape(nb, NIMG, PD)
    order = np.concatenate([np.arange(0, DH, 2), np.arange(1, DH, 2)])
    cols = (np.arange(4)[:, None, None] * P + order[None, :, None] + np.arange(H // 2)[None, None, :] * DH).reshape(-1)
    cols = np.concatenate([cols, np.arange(2 * D, 3 * D)])
    pe, rope, masks, tokens = host_constants()
    a = {
        "patches_tok": p, "patches_T": p.reshape(nb, NIMG, KP, P).transpose(0, 3, 2, 1),
        "txt": i["txt"], "ln1_w": np.asarray(i["L0_tok_ln1_w"]).reshape(KP, P).T, "WT": np.asarray(i["L0_tok_W"]).T,
        "ln2_w": i["L0_tok_ln2_w"], "Wqkv": np.asarray(i["L0_attn_Wqkv"])[:, cols],
        "bqkv": np.asarray(i["L0_attn_bqkv"])[cols], "Wo": i["L0_attn_Wo"], "bo": i["L0_attn_bo"],
        "gamma": i["L0_attn_gamma"], "beta": i["L0_attn_beta"], "Wr": i["L0_ffn_Wr"],
        "W1": i["L0_ffn_W1"], "W2": i["L0_ffn_W2"], "pe": pe, "rope": rope, "masks": masks, "tokens": tokens,
    }
    return {k: np.ascontiguousarray(np.asarray(a[k])) for k in _ORDER}


def kernel(**inputs):
    import concourse.bacc as bacc
    from concourse.bass_utils import run_bass_kernel_spmd as run
    arrays = lay_out(inputs)
    nb = arrays["txt"].shape[0]
    nc = bacc.Bacc("TRN2", target_bir_lowering=False, num_devices=1)
    args = [nc.dram_tensor("in_" + k, arrays[k].shape, mybir.dt.from_np(arrays[k].dtype),
                           kind="ExternalInput").ap() for k in _ORDER]
    out = nc.dram_tensor("out_0", (nb, S, D), F32, kind="ExternalOutput").ap()
    build_program(nc, nb, 364, (122, 121, 121), *args, out)
    r = run(nc, [{"in_" + k: v for k, v in arrays.items()}], core_ids=[0])
    return r.results[0]["out_0"]
```

```python
import numpy as np
import concourse.bass as bass
import concourse.mybir as mybir
from contextlib import ExitStack

F32 = mybir.dt.float32
F32R = mybir.dt.float32r
BF16 = mybir.dt.bfloat16
U32 = mybir.dt.uint32
ALU = mybir.AluOpType
ACT = mybir.ActivationFunctionType
AX = mybir.AxisListType

P = 128
D = 256
H, DH = 16, 16
HP = 32
NTXT = 77
HW = 14
NIMG = HW * HW
S = NIMG + NTXT
PD = 768
KP = PD // P
NE, FF = 8, 1024
GB = 4
NT = 2 * GB + 1
REM = S - 2 * P
IMG1 = NIMG - P
SB_ = 2 * P + 32
GC = GB * SB_
NQ = H // 4
PARTS = 3
KR = 6 * DH
ROW = D + 4
BIG = 65536.0
EPS = 1e-5
Q_RUNS = ((0, 0, 3), (3, 0, 2), (5, 0, 1))
K_RUNS = ((0, 0, 1), (1, 0, 1), (2, 0, 1), (3, 1, 1), (4, 1, 1), (5, 2, 1))
PRING = 8


def at(g, per, k):
    return g * per + (max(k, 0) + 1)


def settle(eng, sem):
    eng.sem_inc(sem, 1)


class Chain:

    def __init__(self, eng, sem, per):
        self.eng, self.sem, self.per, self.k = eng, sem, per, 0

    def start(self, g):
        self.g, self.k = g, 0

    def link(self, ins):
        ins.then_inc(self.sem, 1)
        self.k += 1
        self.eng.wait_ge(self.sem, at(self.g, self.per, self.k))

    def end(self):
        assert self.k == self.per, (self.k, self.per)


def build_program(nc, nb, chunk, cuts, patches_tok, patches_T, txt, ln1_w, WT, ln2_w, Wqkv, bqkv, Wo, bo,
                  gamma, beta, Wr, W1, W2, pe, rope, masks, tokens, out):
    ng = nb // GB
    ntok = nb * S
    cap = -(-ntok // NE)
    nslot = NE * cap
    out_rows = out.rearrange("b s d -> (b s) d")
    xe = nc.dram_tensor("xe", [nslot, ROW], F32, kind="Internal").ap()
    spread = nc.dram_tensor("spread", [4, PARTS * DH, H // 2, GC], BF16, kind="Internal").ap()

    outer = ExitStack()
    sems = []

    def sem(name):
        s = outer.enter_context(nc.semaphore(name))
        sems.append(s)
        return s

    phase_a(nc, sem, ng, cap, nslot, patches_tok, patches_T, txt, ln1_w, WT, ln2_w, Wqkv, bqkv, Wo, bo,
            gamma, beta, Wr, pe, rope, masks, tokens, out, xe, spread)
    phase_b(nc, sem, cap, ntok, chunk, cuts, xe, W1, W2, out_rows)
    outer.close()


def phase_a(nc, sem, ng, cap, nslot, patches_tok, patches_T, txt, ln1_w, WT, ln2_w, Wqkv, bqkv, Wo, bo,
            gamma, beta, Wr, pe, rope, masks, tokens, out, xe, spread):
    ctx = ExitStack()

    def sb(name, shape, dt=F32):
        return ctx.enter_context(nc.sbuf_tensor(name, shape, dt))

    A_sb = sb("A_sb", [P, KP, D])
    csum = sb("csum", [P, D])
    wqkv = sb("wqkv", [P, 2, 3 * D])
    wo = sb("wo", [P, 2, D])
    wr = sb("wr", [P, 2, NE])
    g1 = sb("g1", [P, KP])
    g2 = sb("g2", [P, D])
    pes = sb("pes", [P, 2, D])
    bq = sb("bq", [P, 3 * D])
    bos = sb("bos", [P, D])
    gam = sb("gam", [P, D])
    bet = sb("bet", [P, D])
    rop = sb("rop", [P, 2, 3, DH // 2])
    msk = sb("msk", [P, 24])
    tokr = sb("tokr", [P, NT])
    idf = sb("idf", [P, P])
    idb = sb("idb", [P, P], BF16)
    onesb = sb("onesb", [P, P], BF16)
    before = sb("before", [P, P], BF16)
    fromb = sb("fromb", [P, GB, P], BF16)
    neghalf = sb("neghalf", [P, NT])
    NPT = GB * KP * NIMG
    union = sb("union", [P, NPT + 2 * PD])
    pT = union[:, 0:NPT].rearrange("p (r k n) -> p r k n", r=GB, k=KP)
    ptok = union[:, NPT:NPT + 2 * PD].rearrange("p (r n) -> p r n", r=2)
    prob = union[:, 0:PRING * 2 * S].rearrange("p (r c n) -> p r c n", r=PRING, c=2)
    probr = union[:, PRING * 2 * S:(PRING + 1) * 2 * S].rearrange("p (r n) -> p r n", r=2)
    zz = sb("zz", [P, 4, D])
    st = sb("st", [P, 2, 12])
    st2 = sb("st2", [P, 2, 6])
    mv1 = sb("mv1", [P, 2 * GB, 2])
    nm1 = sb("nm1", [P, 2 * GB])
    ve1 = sb("ve1", [P, 2 * GB])
    rs1 = sb("rs1", [P, 2 * GB])
    mv2 = sb("mv2", [P, 2 * GB, 2])
    ve2 = sb("ve2", [P, 2 * GB])
    rp2 = sb("rp2", [P, 2 * GB])
    rs2 = sb("rs2", [P, 2 * GB])
    hN = sb("hN", [P, NT, D])
    stN = sb("stN", [P, NT, 6])
    mvN = sb("mvN", [P, NT, 2])
    veN = sb("veN", [P, NT])
    rsN = sb("rsN", [P, NT])
    hC = sb("hC", [P, NT, D])
    nmN = sb("nmN", [P, NT])
    mvC = sb("mvC", [P, NT, 2])
    rsC = sb("rsC", [P, NT])
    xn = sb("xn", [P, 2, D])
    xTs = sb("xTs", [P, 2, D])
    qks = sb("qks", [P, 2, 2 * D])
    rot = sb("rot", [P, 2 * D])
    rest = sb("rest", [P, 4, P])
    ones = rest[:, 0, :]
    comp = sb("comp", [P, PARTS, 4, GC], BF16)
    Vflat = sb("Vflat", [P, NT * H * (DH + 1) + HP])
    V = Vflat[:, 0:NT * H * (DH + 1)].rearrange("p (t h d) -> p t h d", t=NT, h=H)
    Vbd = sb("Vbd", [P, GB, NQ, P])
    qh = sb("qh", [P, 2, 4, GC], BF16)
    kh = sb("kh", [P, 2, 4, GC], BF16)
    mxs = sb("mxs", [P, 4, NT])
    cs = sb("cs", [P, NT, 4, PARTS], BF16)
    csr = sb("csr", [P, NT, 4])
    O_sb = sb("O_sb", [P, NQ, 2 * GB * P + GB * 32])
    rd = sb("rd", [P, H])
    an = sb("an", [P, H, DH])
    aTs = sb("aTs", [P, D])
    res = sb("res", [P, 3, D])
    stA = sb("stA", [P, 6])
    mvA = sb("mvA", [P, NT, 2])
    veA = sb("veA", [P, NT])
    rsA = sb("rsA", [P, NT])
    stB = sb("stB", [P, 6])
    veB = sb("veB", [P, NT])
    y = sb("y", [P, 2, D])
    yTs = sb("yTs", [P, D])
    pay = sb("pay", [P, NT, ROW])
    mx8 = sb("mx8", [P, NT, 8])
    ix8 = sb("ix8", [P, NT, 8], U32)
    lsh = sb("lsh", [P, NT, NE])
    psum_e = sb("psum_e", [P, NT])
    ef = sb("ef", [P, NT])
    oh = sb("oh", [P, NT, NE])
    ohb = sb("ohb", [P, NT, NE], BF16)
    ct = sb("ct", [P, NT, NE])
    ctb = sb("ctb", [P, NT, NE], BF16)
    pairb = sb("pairb", [P, GB, NE], BF16)
    totb = sb("totb", [P, NE], BF16)
    base = sb("base", [P, NE])
    rk = lsh
    rks = sb("rks", [P, NT])
    pen = sb("pen", [P, NT])
    slot = sb("slot", [P, NT])
    slotu = sb("slotu", [P, NT], U32)

    def bank(name, n=1):
        return ctx.enter_context(nc.psum_tensor(name, [P, 512 * n], F32))

    b01, b23, b45, b6, b7 = bank("b01", 2), bank("b23", 2), bank("b45", 2), bank("b6"), bank("b7")
    scp = [b[:, :].rearrange("p (c n) -> p c n", c=2) for b in (b23, b45)]
    z_ps = [b23[:, 0:D], b23[:, 512:512 + D]]
    xT_ps = b01[:, 0:D]
    qk_ps = b01[:, 512:1024]
    v_ps = b23[:, 0:D]
    qkT_ps = b23[:, 512:1024]
    oT_ps = b45[:, 0:512]
    wo_ps = b45[:, 512:512 + D]
    aT_ps, yT_ps = b7[:, 0:D], b7[:, D:2 * D]
    lg_ps = b6[:, 0:NT * NE].rearrange("p (t e) -> p t e", e=NE)
    rk_ps = b6[:, 128:128 + NT * NE]
    tot_ps = b6[:, 256:256 + NE]

    const_in = sem("const_in")
    pool_set = sem("pool_set")
    rows_set = sem("rows_set")
    settled = sem("settled")
    A_ready, csum_ready = sem("A_ready"), sem("csum_ready")
    cs_ps = sem("cs_ps")
    credit = []

    def csem(name, dma=False):
        s = sem(name)
        credit.append((s, dma))
        return s

    ptok_in = [csem(f"ptok_in{i}", 1) for i in range(2)]
    pT_in = [csem(f"pT_in{i}", 1) for i in range(GB)]
    txt_in = csem("txt_in", 1)
    ptok_used = csem("ptok_used")
    rs1_in, rs1_ready = csem("rs1_in"), csem("rs1_ready")
    rs2_in, rs2_ready = csem("rs2_in"), csem("rs2_ready")
    z_ready, z_used = csem("z_ready"), csem("z_used")
    zn_ready, emb_ready = csem("zn_ready"), csem("emb_ready")
    rsN_in, rsN_ready = csem("rsN_in"), csem("rsN_ready")
    nmN_ready = csem("nmN_ready")
    hN_taken = csem("hN_taken")
    xn_ready, xT_tr, xT_in = csem("xn_ready"), csem("xT_tr"), csem("xT_in")
    qkv_ready, qkv_used = csem("qkv_ready"), csem("qkv_used")
    rope_done, qkT_ready = csem("rope_done"), csem("qkT_ready")
    hi_ready, parts_ready = csem("hi_ready"), csem("parts_ready")
    vbd_ready = csem("vbd_ready")
    spread_out = [[csem(f"spread_out{c}{f}", 1) for f in range(2)] for c in range(2)]
    hat_in = [[csem(f"hat_in{r}{h}", 1) for h in range(2)] for r in range(2)]
    mx_ready, mx_used = csem("mx_ready"), csem("mx_used")
    cs_ready = csem("cs_ready")
    ct_ready = csem("ct_ready")
    cv_done, ca_done = csem("cv_done"), csem("ca_done")
    s_ready, p_ready = csem("s_ready"), csem("p_ready")
    r_ready, pr_ready = csem("r_ready"), csem("pr_ready")
    pv_done, av_ready, o_used = csem("pv_done"), csem("av_ready"), csem("o_used")
    oT_ready, an_ready = csem("oT_ready"), csem("an_ready")
    aT_ready, aT_in = csem("aT_ready"), csem("aT_in")
    xb_ready = csem("xb_ready")
    wo_ready, wo_used = csem("wo_ready"), csem("wo_used")
    rsA_in, rsA_ready = csem("rsA_in"), csem("rsA_ready")
    h2_ready = csem("h2_ready")
    rsB_in, rsB_ready = csem("rsB_in"), csem("rsB_ready")
    y_ready, yT_ready, yT_in, lg_ready = csem("y_ready"), csem("yT_ready"), csem("yT_in"), csem("lg_ready")
    lsh_ready, le_ready = csem("lsh_ready"), csem("le_ready")
    oh_ready, rk_ready, slot_ready = csem("oh_ready"), csem("rk_ready"), csem("slot_ready")
    outw = csem("outw", 1)
    scat = sem("scat")
    scattered = csem("scattered")
    filled = csem("filled", 1)
    v_stepE, v_stepX, v_stepA, v_stepT, v_stepR = (csem("v_step" + c) for c in "EXATR")
    v_stepP = csem("v_stepP")
    p_stepX, p_stepT, p_stepE = csem("p_stepX"), csem("p_stepT"), csem("p_stepE")

    NFILL = 39
    NE_STEPS = GB + 3
    TAIL = NT + 3
    MAX_STEPS = {TAIL + 1: range(0, 8), TAIL + 2: range(8, 16), TAIL + 3: range(16, 24)}
    M0, M1, M2 = 24, 28, 32
    PATCH_STEPS = (4, 6, 8, 10)
    NHAT = NQ // 2 * (len(Q_RUNS) + len(K_RUNS))
    NCONST = 14
    NWARM, NWARM0 = 1, 3
    NMX = NQ * NT
    block = ctx.enter_context(nc.Block())

    def for_dma(g, per, k):
        return at(g, per, k) * 16

    def max_bank(qd, u):
        bank = b01 if u % 4 < 2 or qd else b45
        return bank[:, u % 2 * 512:u % 2 * 512 + S]

    def max_tile(u):
        if u < 8 * GB:
            return u // 2 % 4, 2 * (u // 8) + u % 2
        return u - 8 * GB, 2 * GB

    def max_rows(qd, i):
        src = b01[KR:KR + PARTS, i % 2 * 512:(i % 2 + 1) * 512].bitcast(BF16)
        dst = qh[KR:KR + PARTS, qd % 2, :, :].rearrange("p j (b n) -> p j b n", b=GB)
        if i == 0:
            return dst[:, :, :, 2 * P:SB_], src[:, 0:4 * P].rearrange("p (j b n) -> p j b n", j=4, b=GB)
        return dst[:, i - 1, :, 0:2 * P], src.rearrange("p (b n) -> p b n", b=GB)

    x_order = (2 * GB, *range(2 * GB))

    def tile_rows(i):
        return P if i % 2 == 0 else IMG1

    def tile_cols(ap, t):
        if t < 2 * GB:
            c0 = (t // 2) * SB_ + (t % 2) * P
            return ap[:, :, c0:c0 + P]
        return ap.rearrange("p f (b n) -> p f b n", b=GB)[:, :, :, 2 * P:SB_]

    @block.sync
    def _(sp):
        for s, dma in credit:
            sp.sem_inc(s, 16 if dma else 1)
        sp.dma_start(g1[:, :], ln1_w).then_inc(const_in, 16)
        sp.dma_start(A_sb[:, :, :], WT.rearrange("(k p) n -> p k n", p=P)).then_inc(const_in, 16)
        sp.dma_start(wqkv[:, :, :], Wqkv.rearrange("(k p) n -> p k n", p=P)).then_inc(const_in, 16)
        sp.dma_start(wo[:, :, :], Wo.rearrange("(k p) n -> p k n", p=P)).then_inc(const_in, 16)
        sp.dma_start(wr[:, :, :], Wr.rearrange("(k p) n -> p k n", p=P)).then_inc(const_in, 16)
        for dst, src in ((g2, ln2_w), (bq, bqkv), (bos, bo), (gam, gamma), (bet, beta)):
            sp.dma_start(dst[:, :], src.partition_broadcast(P)).then_inc(const_in, 16)
        sp.dma_start(pes[:, :, :], pe).then_inc(const_in, 16)
        sp.dma_start(rop[:, :, :, :], rope).then_inc(const_in, 16)
        sp.dma_start(msk[:, :], masks).then_inc(const_in, 16)
        sp.dma_start(tokr[:, :], tokens).then_inc(const_in, 16)
        sp.wait_ge(pool_set, 1)
        per = nslot // (NFILL * 4)
        assert per * NFILL * 4 == nslot and per <= P
        for i in range(NFILL):
            sp.dma_start(xe[i * per * 4:(i + 1) * per * 4, :].rearrange("(p r) n -> p r n", r=4),
                         pay[0:per, 0:4, :]).then_inc(filled, 16)

        def ptok_load(g, b):
            if b >= 1:
                sp.wait_ge(ptok_used, at(g, 8, 2 * b))
                settle(sp, settled)
            for c in range(2):
                r = tile_rows(c)
                sp.dma_start(ptok[0:r, c, :], patches_tok[bass.ds(g * GB + b, 1), c * P:c * P + r, :]
                             .rearrange("a p n -> p (a n)")).then_inc(ptok_in[c], 16)

        def pT_loads(g):
            for b in range(GB):
                sp.dma_start(pT[:, b, :, :], patches_T[bass.ds(g * GB + b, 1), :, :, :]
                             .rearrange("a p k n -> p (a k) n")).then_inc(pT_in[b], 16)

        def hats(g, qd, hb):
            cols = slice(hb * 2 * SB_, (hb + 1) * 2 * SB_)
            heads = slice(4 * (qd % 2), 4 * (qd % 2) + 4)
            for dst, f, runs in ((qh, qd // 2, Q_RUNS), (kh, 2 + qd // 2, K_RUNS)):
                for i, part, n in runs:
                    sp.dma_start(dst[DH * i:DH * (i + n), qd % 2, :, cols],
                                 spread[f, DH * part:DH * (part + n), heads, cols]).then_inc(hat_in[qd % 2][hb], 16)

        def spreads(g, hb):
            for ready in (hi_ready, parts_ready):
                sp.wait_ge(ready, at(g, 9, 5 + 4 * hb))
                settle(sp, settled)
            cols = slice(hb * 2 * SB_, (hb + 1) * 2 * SB_)
            for f in (0, 2, 1, 3):
                sp.dma_start(spread[f, :, :, cols].rearrange("(a d) h t -> (d h) a t", a=PARTS), comp[:, :, f, cols]
                             ).then_inc(spread_out[hb][f % 2], 16)
            sp.wait_ge(spread_out[hb][0], for_dma(g, 2, 2))
            settle(sp, settled)
            for qd in range(2):
                hats(g, qd, hb)

        def attn(g, nxt, emb):
            for qd in (2, 3):
                for hb in range(2):
                    sp.wait_ge(spread_out[hb][1], for_dma(g, 2, 2))
                    settle(sp, settled)
                    sp.wait_ge(r_ready, at(g, 16, (qd - 2) * GB + 2 * hb + 2))
                    settle(sp, settled)
                    hats(g, qd, hb)
            if emb:
                sp.wait_ge(av_ready, at(g, 16, 16))
                settle(sp, settled)
                ptok_load(g + 2, 0)
                pT_loads(g + 2)
                ptok_load(g + 2, 1)
                ptok_load(g + 2, 2)
            if nxt:
                spreads(g + 1, 0)
            if emb:
                ptok_load(g + 2, 3)
            if nxt:
                spreads(g + 1, 1)
            sp.wait_ge(h2_ready, at(g, 9, 9))
            settle(sp, settled)
            for b in range(GB):
                sp.dma_start(out[bass.ds(g * GB + b, 1), 0:2 * P, :].rearrange("a (c p) d -> p (a c) d", p=P),
                             pay[:, 2 * b:2 * b + 2, 0:D]).then_inc(outw, 16)
                sp.dma_start(out[bass.ds(g * GB + b, 1), 2 * P:S, :].rearrange("a p d -> p (a d)"),
                             pay[32 * b:32 * b + REM, 2 * GB, 0:D]).then_inc(outw, 16)

        sp.wait_ge(pool_set, 2)
        for g in range(2):
            if g == 1:
                sp.wait_ge(z_ready, at(1, 8, 0))
                sp.wait_ge(ptok_used, at(1, 8, 0))
            ptok_load(g, 0)
            pT_loads(g)
            for b in range(1, GB):
                ptok_load(g, b)
            if g == 0:
                spreads(0, 0)
                spreads(0, 1)
        with sp.Fori(0, ng - 2) as g:
            attn(g, True, True)
        attn(ng - 2, True, False)
        attn(ng - 1, False, False)
        sp.wait_ge(outw, 16 * at(ng, 8, 0))

    @block.scalar
    def _(act):
        def text_loads(g):
            act.wait_ge(hN_taken, at(g, 1, 0))
            for b in range(GB):
                act.dma_start(hN[IMG1:P, 2 * b + 1, :], txt[bass.ds(g * GB + b, 1), 0:P - IMG1, :]
                              .rearrange("a p d -> p (a d)")).then_inc(txt_in, 16)
                act.dma_start(hN[32 * b:32 * b + REM, 2 * GB, :], txt[bass.ds(g * GB + b, 1), P - IMG1:NTXT, :]
                              .rearrange("a p d -> p (a d)")).then_inc(txt_in, 16)

        def x_norm(g, t):
            if t == 0:
                act.wait_ge(nmN_ready, at(g, 1, 1))
            act.wait_ge(xT_tr, at(g, 9, t - 1))
            c = x_order[t]
            act.activation(xn[:, t % 2, :], hN[:, c, :], ACT.Identity, bias=nmN[:, c:c + 1],
                           scale=rsN[:, c:c + 1]).then_inc(xn_ready, 1)

        def x_tile_a(g, t):
            act.wait_ge(qkv_ready, at(g, 9, t - 1))
            act.wait_ge(xT_tr, at(g, 9, t + 1))
            act.activation(xTs[:, t % 2, :], xT_ps, ACT.Copy).then_inc(xT_in, 1)

        def x_tile_b(g, t):
            if t == 0:
                for place in hat_in[0] + hat_in[1]:
                    act.wait_ge(place, for_dma(g, NHAT, 0))
            act.wait_ge(qkT_ready, at(g, 9, t + 1))
            src = qkT_ps.rearrange("p (f n) -> p f n", f=4)
            c = x_order[t]
            if c == 2 * GB:
                src = qkT_ps.rearrange("p (f b n) -> p f b n", f=4, b=GB)
            act.activation(tile_cols(comp[:, 0], c), src, ACT.Copy).then_inc(hi_ready, 1)

        def t_tile_a(g, t):
            act.wait_ge(wo_ready, at(g, 9, t))
            act.wait_ge(aT_ready, at(g, 9, t + 1))
            act.activation(aTs[:, :], aT_ps, ACT.Copy).then_inc(aT_in, 1)

        def t_tile_b(g, t):
            act.wait_ge(lg_ready, at(g, 9, t))
            act.wait_ge(yT_ready, at(g, 9, t + 1))
            act.activation(yTs[:, :], yT_ps, ACT.Copy).then_inc(yT_in, 1)

        def run(g):
            for s in range(NT + 3):
                if s < NT:
                    x_norm(g, s)
                if 1 <= s < NT + 1:
                    x_tile_a(g, s - 1)
                if 3 <= s < NT + 3:
                    x_tile_b(g, s - 3)

        def c_rows(g, qd, i):
            act.wait_ge(ct_ready, at(g, 5 * NQ, 5 * qd + i + 1))
            dst, src = max_rows(qd, i)
            act.activation(dst, src, ACT.Copy).then_inc(ca_done, 1)

        def o_out(g, qd, b):
            act.wait_ge(av_ready, at(g, 16, qd * GB + b + 1))
            act.activation(O_sb[:, qd, b * 2 * P:(b + 1) * 2 * P], b7[:, 0:2 * P], ACT.Copy)
            act.activation(O_sb[:, qd, 2 * GB * P + 32 * b:2 * GB * P + 32 * b + REM], b7[:, 2 * P:S], ACT.Copy
                           ).then_inc(o_used, 1)

        def attn(g, nxt, emb):
            if nxt:
                act.wait_ge(z_ready, at(g + 1, 8, 8))
                act.wait_ge(ptok_used, at(g + 1, 8, 8))
            act.wait_ge(qkv_used, at(g, 9, 9))
            for b in range(GB):
                for j in range(4):
                    last = act.activation(Vbd[32 * j:32 * j + 32, b, :, 32 * j:32 * j + DH + 1],
                                          V[32 * b:32 * b + 32, 2 * GB, j:H:4, :], ACT.Copy)
            last.then_inc(vbd_ready, 1)
            act.wait_ge(oT_ready, at(g, 9, 0))
            c_rows(g, 0, 2)
            c_rows(g, 0, 4)
            for qd in range(NQ):
                for b in range(GB):
                    for j in range(4):
                        n = (qd * GB + b) * 4 + j
                        act.wait_ge(s_ready, at(g, 64, n + 1))
                        act.wait_ge(pv_done, at(g, 16, (n - PRING) // 4 + 1 if n >= PRING else 0))
                        act.activation(prob[:, n % PRING, :, :], scp[n % 2][:, :, 0:S], ACT.Exp,
                                       scale=float(DH) ** -0.5).then_inc(p_ready, 1)
                        if j == 2 and b >= 1:
                            o_out(g, qd, b - 1)
                    m = qd * GB + b
                    act.wait_ge(r_ready, at(g, 16, m + 1))
                    act.wait_ge(av_ready, at(g, 16, m - 1 if m >= 2 else 0))
                    act.activation(probr[:, m % 2, :], b6[:, 0:S], ACT.Exp,
                                   scale=float(DH) ** -0.5).then_inc(pr_ready, 1)
                if qd + 1 < NQ:
                    c_rows(g, qd + 1, 2)
                o_out(g, qd, GB - 1)
                if qd + 1 < NQ:
                    c_rows(g, qd + 1, 4)
            for s in range(NT + 7):
                if nxt and s < NT:
                    x_norm(g + 1, s)
                if nxt and 1 <= s < NT + 1:
                    x_tile_a(g + 1, s - 1)
                if 1 <= s < NT + 1:
                    t_tile_a(g, s - 1)
                if nxt and 3 <= s < NT + 3:
                    x_tile_b(g + 1, s - 3)
                if 6 <= s < NT + 6:
                    t_tile_b(g, s - 6)
            if emb:
                text_loads(g + 2)
            act.wait_ge(lsh_ready, at(g, 1, 1))
            act.activation(lsh[:, :, :], lsh[:, :, :], ACT.Exp).then_inc(le_ready, 1)

        act.wait_ge(pool_set, 2)
        text_loads(0)
        run(0)
        text_loads(1)
        with act.Fori(0, ng - 2) as g:
            attn(g, True, True)
        attn(ng - 2, True, False)
        attn(ng - 1, False, False)

    @block.gpsimd
    def _(pool):
        pool.memset(pay[:, 0:4, 0:ROW - 1], 0.0)
        pool.memset(pay[:, 0:4, ROW - 1:ROW], BIG).then_inc(pool_set, 1)
        pool.memset(idf[:, :], 0.0)
        pool.memset(idb[:, :], 0.0)
        pool.memset(onesb[:, :], 1.0)
        pool.memset(ones, 1.0)
        pool.memset(before[:, :], 1.0)
        pool.memset(fromb[:, :, :], 1.0)
        pool.memset(neghalf[:, :], -0.5)
        pool.memset(hN[:, :, :], 0.0)
        pool.memset(Vflat[:, :], 1.0)
        pool.memset(Vbd[:, :, :, :], 0.0)
        pool.memset(O_sb[:, :, :], 1.0)
        pool.memset(base[:, :], 0.0).then_inc(pool_set, 1)
        pool.wait_ge(pool_set, 2)
        for m in (idf, idb):
            pool.affine_select(out=m[:, :], in_=m[:, :], compare_op=ALU.not_equal, fill=1.0, base=0,
                               pattern=[[-1, P]], channel_multiplier=1)
        pool.affine_select(out=before[:, :], in_=before[:, :], compare_op=ALU.is_gt, fill=0.0, base=0,
                           pattern=[[1, P]], channel_multiplier=-1)
        for b in range(GB):
            last = pool.affine_select(out=fromb[:, b, :], in_=fromb[:, b, :], compare_op=ALU.is_ge, fill=0.0,
                                      base=-32 * b, pattern=[[1, P]], channel_multiplier=0)
        last.then_inc(pool_set, 1)
        pool.wait_ge(const_in, 16 * NCONST)
        pool.wait_ge(pool_set, 3)
        pool.tensor_scalar(V[:, 2 * GB, :, DH], V[:, 2 * GB, :, DH], msk[:, 0:1], 1.0, ALU.mult, ALU.mult
                           ).then_inc(pool_set, 1)

        ex = Chain(pool, p_stepE, 8)
        xx = Chain(pool, p_stepX, 3 * NT)
        tt = Chain(pool, p_stepT, 2 * NT)

        def inv_sqrt(dst, src, n, need, made, value):
            pool.wait_ge(need, value)
            pool.tensor_tensor(dst, src, neghalf[0:dst.shape[0], 0:n], ALU.pow).then_inc(made, 1)

        def e_patches(g, p):
            if p < GB:
                inv_sqrt(rs1[:, 2 * p:2 * p + 2], ve1[:, 2 * p:2 * p + 2], 2, rs1_in, rs1_ready, at(g, GB, p + 1))

        def e_step(g, p):
            if p == 0:
                ex.start(g)
            if 1 <= p < GB + 1:
                q = p - 1
                inv_sqrt(rp2[:, 2 * q:2 * q + 2], ve2[:, 2 * q:2 * q + 2], 2, rs2_in, rs2_ready, at(g, GB, q + 1))
            if 2 <= p < GB + 2:
                for i in (2 * (p - 2), 2 * (p - 2) + 1):
                    r = tile_rows(i)
                    pool.wait_ge(zn_ready, at(g, 8, i + 1))
                    if i == 0:
                        pool.wait_ge(hN_taken, at(g, 1, 0))
                    ex.link(pool.tensor_tensor(zz[0:r, i % 4, :], zz[0:r, i % 4, :], g2[0:r, :], ALU.mult))
                    pool.tensor_tensor(hN[0:r, i, :], zz[0:r, i % 4, :], pes[0:r, i % 2, :], ALU.add
                                       ).then_inc(emb_ready, 1)
            if p == NE_STEPS - 1:
                ex.end()
                inv_sqrt(rsN[:, :], veN[:, :], NT, rsN_in, rsN_ready, at(g, 1, 1))

        def e_stage(g):
            for p in range(NE_STEPS):
                e_patches(g, p)
                e_step(g, p)

        def rope_tile(g, t):
            pool.wait_ge(qkv_used, at(g, 9, t + 1))
            c = x_order[t]
            kind = 2 if c == 2 * GB else c % 2
            x4 = qks[:, t % 2, :].rearrange("p (s a m) -> p s a m", s=4, a=2)
            r4 = rot[:, :].rearrange("p (s a m) -> p s a m", s=4, a=2)
            x3 = qks[:, t % 2, :].rearrange("p (s d h) -> p s d h", s=8, d=DH // 2)

            def table(i, n):
                return rop[:, i, kind, :].unsqueeze(1).unsqueeze(3).broadcast_to([P, n, DH // 2, H // 2])

            def half(ap, a):
                return ap[:, :, a, :].rearrange("p s (d h) -> p s d h", d=DH // 2)

            pool.tensor_tensor(half(r4, 0), half(x4, 1), table(1, 4), ALU.mult)
            xx.link(pool.tensor_tensor(half(r4, 1), half(x4, 0), table(1, 4), ALU.mult))
            xx.link(pool.tensor_tensor(x3, x3, table(0, 8), ALU.mult))
            pool.tensor_tensor(x4[:, :, 0, :], x4[:, :, 0, :], r4[:, :, 0, :], ALU.subtract)
            xx.link(pool.tensor_tensor(x4[:, :, 1, :], x4[:, :, 1, :], r4[:, :, 1, :], ALU.add))
            pool.sem_inc(rope_done, 1)

        def attn(g, nxt, emb):
            tt.start(g)
            pool.wait_ge(hN_taken, at(g, 1, 1))
            pool.wait_ge(filled, for_dma(0, 0, NFILL))
            pool.wait_ge(scattered, at(g, 1, 0))
            pool.wait_ge(outw, for_dma(g, 8, 0))
            for t in range(NT):
                x, h = pay[:, t, 0:D], hC[:, t, :]
                settle(pool, settled)
                tt.link(pool.tensor_scalar(x, h, mvC[:, t, 0:1], rsC[:, t:t + 1], ALU.subtract, ALU.mult))
                pool.tensor_tensor(h, h, bet[:, :], ALU.add)
                tt.link(pool.tensor_tensor(x, x, bos[:, :], ALU.add))
                pool.sem_inc(xb_ready, 1)
            tt.end()
            if nxt:
                xx.start(g + 1)
            for s in range(NT + 7):
                if nxt and 2 <= s < NT + 2:
                    rope_tile(g + 1, s - 2)
                if 2 <= s < NT + 2:
                    t = s - 2
                    inv_sqrt(rsA[:, t:t + 1], veA[:, t:t + 1], 1, rsA_in, rsA_ready, at(g, 9, t + 1))
                if 4 <= s < NT + 4:
                    t = s - 4
                    inv_sqrt(pay[:, t, D + 1:D + 2], veB[:, t:t + 1], 1, rsB_in, rsB_ready, at(g, 9, t + 1))
                if emb and s in PATCH_STEPS:
                    e_patches(g + 2, PATCH_STEPS.index(s))
                if emb and s >= TAIL:
                    e_step(g + 2, s - TAIL)
            if nxt:
                xx.end()
            if emb:
                for p in range(NT + 7 - TAIL, NE_STEPS):
                    e_step(g + 2, p)
            pool.wait_ge(slot_ready, at(g, 1, 1))
            settle(pool, settled)
            for t in range(NT):
                pool.indirect_dma_start(out=xe, out_offset=bass.IndirectOffsetOnAxis(ap=slotu[:, t:t + 1], axis=0),
                                        in_=pay[:, t, :], in_offset=None, bounds_check=nslot - 1,
                                        oob_is_err=False).then_inc(scat, 16)
            pool.wait_ge(scat, 16 * NT * (g + 1))
            pool.sem_inc(scattered, 1)

        e_stage(0)
        xx.start(0)
        for t in range(NT):
            rope_tile(0, t)
        xx.end()
        e_stage(1)
        with pool.Fori(0, ng - 2) as g:
            attn(g, True, True)
        attn(ng - 2, True, False)
        attn(ng - 1, False, False)

    @block.vector
    def _(dve):
        ce = Chain(dve, v_stepE, 6 * GB + 2)
        cx = Chain(dve, v_stepX, 2)
        cp = Chain(dve, v_stepP, 2 * NT)
        ca = Chain(dve, v_stepA, 4 * 4)
        ctn = Chain(dve, v_stepT, 6 * NT + 4)
        cr = Chain(dve, v_stepR, 0)

        dve.memset(mv1[:, :, :], 1.0)
        dve.memset(mv2[:, :, :], 1.0)
        dve.memset(qh[KR:P, :, :, :], 0.0)
        dve.memset(kh[KR:P, :, :, :], 0.0).then_inc(rows_set, 1)
        dve.wait_ge(rows_set, 1)
        ones_rows = kh[KR:KR + PARTS, :, :, :].rearrange("p r j (b n) -> p (r j) b n", b=GB)
        dve.memset(ones_rows[:, :, :, 0:S], 1.0)
        dve.wait_ge(const_in, 16 * NCONST)
        for k in range(KP):
            last = dve.tensor_scalar(A_sb[:, k, :], A_sb[:, k, :], g1[:, k:k + 1], None, ALU.mult)
        last.then_inc(A_ready, 1)
        dve.wait_ge(cs_ps, 1)
        dve.tensor_copy(csum[:, :], b6[:, 0:D]).then_inc(csum_ready, 1)
        dve.wait_ge(csum_ready, 1)
        dve.wait_ge(pool_set, 4)

        def e_patches(g, p):
            if p == 0:
                ce.start(g)
            if p < GB:
                for c in range(2):
                    r = tile_rows(c)
                    dve.wait_ge(ptok_in[c], for_dma(g, 4, p + 1))
                    pt = ptok[0:r, c, :].rearrange("p (a n) -> p a n", a=2)
                    dve.bn_stats(st[0:r, c, 0:6], pt[:, 0, :])
                    dve.bn_stats(st[0:r, c, 6:12], pt[:, 1, :]).then_inc(ptok_used, 1)
                dve.wait_ge(ptok_used, at(g, 8, 2 * p + 2))
                settle(dve, settled)
                for c in range(2):
                    r = tile_rows(c)
                    last = dve.bn_aggr(mv1[0:r, 2 * p + c, :], st[0:r, c, :])
                ce.link(last)
                pair = slice(2 * p, 2 * p + 2)
                dve.tensor_scalar(ve1[:, pair], mv1[:, pair, 1], EPS, None, ALU.add).then_inc(rs1_in, 1)
                ce.link(dve.tensor_scalar(nm1[:, pair], mv1[:, pair, 0], -1.0, None, ALU.mult))

        def e_step(g, p):
            if 1 <= p < GB + 1:
                q = p - 1
                for i in (2 * q, 2 * q + 1):
                    r = tile_rows(i)
                    zi = zz[0:r, i % 4, :]
                    dve.wait_ge(emb_ready, at(g, 8, i - 3))
                    dve.wait_ge(z_ready, at(g, 8, i + 1))
                    dve.scalar_tensor_tensor(zi, csum[0:r, :], nm1[0:r, i:i + 1], z_ps[i % 2][0:r, :],
                                             ALU.mult, ALU.add).then_inc(z_used, 1)
                    dve.wait_ge(z_used, at(g, 8, i + 1))
                    last = dve.bn_stats(st2[0:r, i % 2, :], zi)
                ce.link(last)
                settle(dve, settled)
                for i in (2 * q, 2 * q + 1):
                    r = tile_rows(i)
                    last = dve.bn_aggr(mv2[0:r, i, :], st2[0:r, i % 2, :])
                ce.link(last)
                dve.wait_ge(rs1_ready, at(g, GB, q + 1))
                for i in (2 * q, 2 * q + 1):
                    last = dve.tensor_scalar(ve2[:, i:i + 1], mv2[:, i, 1:2], rs1[:, i:i + 1], rs1[:, i:i + 1],
                                             ALU.mult, ALU.mult)
                ce.link(last)
                pair = slice(2 * q, 2 * q + 2)
                dve.tensor_scalar(ve2[:, pair], ve2[:, pair], EPS, None, ALU.add).then_inc(rs2_in, 1)
            if 2 <= p < GB + 2:
                q = p - 2
                pair = slice(2 * q, 2 * q + 2)
                dve.wait_ge(rs2_ready, at(g, GB, q + 1))
                ce.link(dve.tensor_tensor(rs2[:, pair], rp2[:, pair], rs1[:, pair], ALU.mult))
                for i in (2 * q, 2 * q + 1):
                    r = tile_rows(i)
                    zi = zz[0:r, i % 4, :]
                    dve.tensor_scalar(zi, zi, mv2[0:r, i, 0:1], rs2[0:r, i:i + 1], ALU.subtract, ALU.mult
                                      ).then_inc(zn_ready, 1)
            if p >= 3:
                q = p - 3
                if q == 0:
                    dve.wait_ge(txt_in, for_dma(g, 8, 8))
                dve.wait_ge(emb_ready, at(g, 8, 2 * q + 2))
                for t in (2 * q, 2 * q + 1) + ((2 * GB,) if p == NE_STEPS - 1 else ()):
                    last = dve.bn_stats(stN[:, t, :], hN[:, t, :])
            if p == NE_STEPS - 1:
                ce.link(last)
                settle(dve, settled)
                for t in range(NT):
                    last = dve.bn_aggr(mvN[:, t, :], stN[:, t, :])
                ce.link(last)
                dve.tensor_scalar(veN[:, :], mvN[:, :, 1], EPS, None, ALU.add).then_inc(rsN_in, 1)
                ce.end()

        def e_stage(g):
            for p in range(NE_STEPS):
                e_patches(g, p)
                e_step(g, p)

        def x_shift(g):
            dve.wait_ge(rsN_ready, at(g, 1, 1))
            dve.scalar_tensor_tensor(nmN[:, :], mvN[:, :, 0], -1.0, rsN[:, :], ALU.mult, ALU.mult
                                     ).then_inc(nmN_ready, 1)

        def x_bias(g, t):
            dve.wait_ge(qkv_ready, at(g, 9, t + 1))
            dve.wait_ge(qkT_ready, at(g, 9, t - 1))
            qk = qks[:, t % 2, :]
            c = x_order[t]
            v = V[:, c, :, 0:DH]
            dve.tensor_tensor(qk, qk_ps, bq[:, 0:2 * D], ALU.add)
            ins = dve.tensor_tensor(v, v_ps.rearrange("p (h d) -> p h d", d=DH),
                                    bq[:, 2 * D:3 * D].rearrange("p (h d) -> p h d", d=DH), ALU.add)
            if c == 2 * GB:
                cx.link(ins)
                dve.tensor_scalar(qk, qk, msk[:, 0:1], None, ALU.mult)
                ins = dve.tensor_scalar(v, v, msk[:, 0:1], None, ALU.mult)
            ins.then_inc(qkv_used, 1)

        def x_parts(g, t, u=None):
            if t is not None:
                if t == 0:
                    for place in hat_in[0] + hat_in[1]:
                        dve.wait_ge(place, for_dma(g, NHAT, 0))
                dve.wait_ge(hi_ready, at(g, 9, t + 1))
                c = x_order[t]
                shape, kw = ("p (f b n) -> p f b n", {"f": 4, "b": GB}) if c == 2 * GB else ("p (f n) -> p f n", {"f": 4})
                whole = qkT_ps.rearrange(shape, **kw)
                r = rest[:, :, :].rearrange("p f n -> p (f n)").rearrange(shape, **kw)
                high, mid, low = (tile_cols(comp[:, i], c) for i in range(3))
                pieces = [slice(i, i + 1) for i in range(4)] if c == 2 * GB else [slice(0, 4)]
                for f in pieces:
                    last = dve.tensor_tensor(r[:, f], whole[:, f], high[:, f], ALU.subtract)
            if u is not None:
                tg = g - 1 if t is not None else g
                dve.wait_ge(rsA_ready, at(tg, 9, u + 1))
                a = res[:, u % 3, :]
                last = dve.scalar_tensor_tensor(a, a, mvA[:, u, 0:1], gam[:, :], ALU.subtract, ALU.mult)
            chain = cp if u is None else ctn
            chain.link(last)
            if t is not None:
                for f in pieces:
                    last = dve.tensor_copy(mid[:, f], r[:, f])
            if u is not None:
                last = dve.scalar_tensor_tensor(pay[:, u, 0:D], a, rsA[:, u:u + 1], hC[:, u, :], ALU.mult, ALU.add)
            chain.link(last)
            if u is not None:
                dve.sem_inc(h2_ready, 1)
            if t is not None:
                for f in pieces:
                    last = dve.tensor_tensor(low[:, f], r[:, f], mid[:, f], ALU.subtract)
                last.then_inc(parts_ready, 1)

        def t_norm(g, t):
            dve.wait_ge(oT_ready, at(g, 9, t + 1))
            o3 = oT_ps.rearrange("p (h d) -> p h d", d=HP)
            ctn.link(dve.reciprocal(rd[:, :], o3[:, :, DH]))
            dve.wait_ge(aT_ready, at(g, 9, t))
            dve.tensor_tensor(an[:, :, :], o3[:, :, 0:DH],
                              rd[:, :].unsqueeze(2).broadcast_to([P, H, DH]), ALU.mult
                              ).then_inc(an_ready, 1)

        def t_sums(g, t, u):
            if t is not None:
                dve.wait_ge(wo_ready, at(g, 9, t + 1))
                dve.wait_ge(xb_ready, at(g, 9, t + 1))
                dve.wait_ge(h2_ready, at(g, 9, t - 2 if t >= 3 else 0))
                r = res[:, t % 3, :]
                last = dve.tensor_tensor(r, wo_ps, pay[:, t, 0:D], ALU.add)
            if u is not None:
                dve.wait_ge(h2_ready, at(g, 9, u + 1))
                last = dve.bn_stats(stB[:, :], pay[:, u, 0:D])
            ctn.link(last)
            if t is not None:
                dve.sem_inc(wo_used, 1)
                last = dve.bn_stats(stA[:, :], r)
            else:
                settle(dve, settled)
            if u is not None:
                last = dve.bn_aggr(pay[:, u, D:D + 2], stB[:, :])
            ctn.link(last)
            if u is not None:
                dve.tensor_scalar(veB[:, u:u + 1], pay[:, u, D + 1:D + 2], EPS, None, ALU.add).then_inc(rsB_in, 1)
            else:
                settle(dve, settled)
            if t is not None:
                ctn.link(dve.bn_aggr(mvA[:, t, :], stA[:, :]))
                dve.tensor_scalar(veA[:, t:t + 1], mvA[:, t, 1:2], EPS, None, ALU.add).then_inc(rsA_in, 1)

        def t_y(g, t):
            dve.wait_ge(rsB_ready, at(g, 9, t + 1))
            dve.wait_ge(yT_ready, at(g, 9, t - 1))
            dve.tensor_scalar(y[:, t % 2, :], pay[:, t, 0:D], pay[:, t, D:D + 1], pay[:, t, D + 1:D + 2],
                              ALU.subtract, ALU.mult).then_inc(y_ready, 1)

        def take(g):
            dve.wait_ge(xn_ready, at(g, 9, 9))
            dve.tensor_copy(hC[:, :, :], hN[:, :, :])
            dve.tensor_copy(mvC[:, :, :], mvN[:, :, :])
            cx.link(dve.tensor_copy(rsC[:, :], rsN[:, :]))
            dve.sem_inc(hN_taken, 1)

        def run(g):
            cx.start(g)
            x_shift(g)
            cp.start(g)
            for s in range(NT + 3):
                if 2 <= s < NT + 2:
                    x_bias(g, s - 2)
                if 3 <= s < NT + 3:
                    x_parts(g, s - 3)
            take(g)
            cx.end()

        def maxima(g, qd, tiles):
            for u in tiles:
                j, t = max_tile(u)
                dve.wait_ge(mx_ready, at(g, NQ * NMX, qd * NMX + u + 1))
                dve.tensor_reduce(mxs[:, j, t:t + 1], max_bank(qd, u), AX.X, ALU.max).then_inc(mx_used, 1)

        def attn(g, nxt, emb):
            if nxt:
                x_shift(g + 1)
            ca.start(g)
            for qd in range(NQ):
                if qd:
                    maxima(g, qd, range(NMX))
                dve.wait_ge(mx_used, at(g, NQ * NMX, (qd + 1) * NMX))
                dve.wait_ge(ct_ready, at(g, 5 * NQ, 5 * qd))
                mt = mxs[:, :, :].rearrange("p j t -> p t j")
                ca.link(dve.tensor_scalar(cs[:, :, :, 0], mt, -1.0, None, ALU.mult))
                ca.link(dve.scalar_tensor_tensor(csr[:, :, :], mt, -1.0, cs[:, :, :, 0], ALU.mult, ALU.subtract))
                ca.link(dve.tensor_copy(cs[:, :, :, 1], csr[:, :, :]))
                ca.link(dve.tensor_tensor(cs[:, :, :, 2], csr[:, :, :], cs[:, :, :, 1], ALU.subtract))
                dve.sem_inc(cs_ready, 1)
                for i in (0, 1, 3):
                    dve.wait_ge(ct_ready, at(g, 5 * NQ, 5 * qd + i + 1))
                    dst, src = max_rows(qd, i)
                    if i:
                        dve.tensor_copy(dst, src).then_inc(cv_done, 1)
                    else:
                        for j in range(4):
                            last = dve.tensor_copy(dst[:, j], src[:, j])
                        last.then_inc(cv_done, 1)
            ca.end()
            ctn.start(g)
            if nxt:
                cx.start(g + 1)
            for s in range(NT + 7):
                if s < NT:
                    t_norm(g, s)
                if nxt and 2 <= s < NT + 2:
                    if s == 2:
                        dve.wait_ge(av_ready, at(g, 16, 16))
                        dve.wait_ge(vbd_ready, at(g, 1, 1))
                    x_bias(g + 1, s - 2)
                if 2 <= s < NT + 4:
                    t_sums(g, s - 2 if s < NT + 2 else None, s - 4 if s >= 4 else None)
                if 3 <= s < NT + 3:
                    if nxt:
                        x_parts(g + 1, s - 3, s - 3)
                    else:
                        x_parts(g, None, s - 3)
                if 5 <= s < NT + 5:
                    t_y(g, s - 5)
                if nxt and s == TAIL:
                    dve.wait_ge(h2_ready, at(g, 9, 9))
                    take(g + 1)
                    cx.end()
                if emb and s in PATCH_STEPS:
                    e_patches(g + 2, PATCH_STEPS.index(s))
                if emb and s >= TAIL:
                    e_step(g + 2, s - TAIL)
                if nxt and s in MAX_STEPS:
                    maxima(g + 1, 0, MAX_STEPS[s])
            ctn.end()
            route_1(g)
            if emb:
                e_step(g + 2, GB)
            if nxt:
                maxima(g + 1, 0, range(M0, M1))
            route_2(g)
            if emb:
                e_step(g + 2, GB + 1)
            if nxt:
                maxima(g + 1, 0, range(M1, M2))
            if emb:
                e_step(g + 2, GB + 2)
            if nxt:
                maxima(g + 1, 0, range(M2, NMX))

        def route_1(g):
            cr.start(g)
            dve.wait_ge(lg_ready, at(g, 9, 9))
            settle(dve, settled)
            for t in range(NT):
                last = dve.max(mx8[:, t, :], lg_ps[:, t, :])
            cr.link(last)
            settle(dve, settled)
            for t in range(NT):
                last = dve.max_index(ix8[:, t, :], mx8[:, t, :], lg_ps[:, t, :])
            cr.link(last)
            dve.tensor_tensor(lsh[:, :, :], lg_ps, mx8[:, :, 0:1].broadcast_to([P, NT, NE]), ALU.subtract
                              ).then_inc(lsh_ready, 1)
            cr.link(dve.tensor_copy(ef[:, :], ix8[:, :, 0]))
            iota = msk[:, 8:16].unsqueeze(1).broadcast_to([P, NT, NE])
            cr.link(dve.tensor_tensor(oh[:, :, :], iota, ef[:, :].unsqueeze(2).broadcast_to([P, NT, NE]),
                                      ALU.is_equal))
            cr.link(dve.tensor_scalar(oh[:, 2 * GB, :], oh[:, 2 * GB, :], msk[:, 0:1], None, ALU.mult))
            dve.tensor_copy(ohb[:, :, :], oh[:, :, :])
            cr.link(dve.memset(ct[:, 0, :], 0.0))
            for t in range(1, 2 * GB):
                cr.link(dve.tensor_tensor(ct[:, t, :], ct[:, t - 1, :], oh[:, t - 1, :], ALU.add))
            cr.link(dve.memset(ct[:, 2 * GB, :], 0.0))
            for b in range(1, GB):
                last = dve.scalar_tensor_tensor(
                    ct[:, 2 * b:2 * b + 2, :],
                    oh[:, 2 * GB, :].unsqueeze(1).broadcast_to([P, 2, NE]),
                    msk[:, b:b + 1], ct[:, 2 * b:2 * b + 2, :], ALU.mult, ALU.add)
            cr.link(last)
            pr = oh[:, 0:2 * GB, :].rearrange("p (b c) e -> p b c e", c=2)
            dve.tensor_tensor(pairb[:, :, :], pr[:, :, 0, :], pr[:, :, 1, :], ALU.add)
            with nc.allow_low_precision(reason="counts up to 9 are exact in bfloat16"):
                dve.tensor_reduce(totb[:, :], oh[:, :, :].rearrange("p t e -> p e t"), AX.X, ALU.add)
            dve.tensor_copy(ctb[:, :, :], ct[:, :, :]).then_inc(oh_ready, 1)
            dve.wait_ge(le_ready, at(g, 1, 1))
            cr.link(dve.tensor_reduce(psum_e[:, :], lsh[:, :, :], AX.X, ALU.add))
            cr.link(dve.reciprocal(pay[:, :, D + 2], psum_e[:, :]))

        def route_2(g):
            dve.wait_ge(rk_ready, at(g, 1, 1))
            cr.link(dve.tensor_tensor(rk[:, :, :], rk_ps.rearrange("p (t e) -> p t e", e=NE),
                                      base[:, :].unsqueeze(1).broadcast_to([P, NT, NE]), ALU.add))
            cr.link(dve.tensor_tensor(rk[:, :, :], rk[:, :, :], oh[:, :, :], ALU.mult))
            cr.link(dve.tensor_reduce(rks[:, :], rk[:, :, :], AX.X, ALU.add))
            dve.tensor_tensor(base[:, :], base[:, :], tot_ps, ALU.add)
            dve.tensor_scalar(pen[:, :], rks[:, :], float(cap), BIG, ALU.is_ge, ALU.mult)
            cr.link(dve.scalar_tensor_tensor(slot[:, :], ef[:, :], float(cap), rks[:, :], ALU.mult, ALU.add))
            cr.link(dve.tensor_tensor(slot[:, :], slot[:, :], pen[:, :], ALU.add))
            cr.link(dve.tensor_scalar(slot[:, 2 * GB:NT], slot[:, 2 * GB:NT], msk[:, 4:5], None, ALU.add))
            dve.wait_ge(scattered, at(g, 1, 0))
            cr.link(dve.tensor_copy(slotu[:, :], slot[:, :]))
            cr.link(dve.tensor_copy(pay[:, :, D + 3], tokr[:, :]))
            cr.link(dve.tensor_scalar(tokr[:, :], tokr[:, :], float(GB * S), None, ALU.add))
            dve.sem_inc(slot_ready, 1)
            cr.end()

        cr.per = 26
        e_stage(0)
        run(0)
        maxima(0, 0, range(NMX))
        e_stage(1)
        with dve.Fori(0, ng - 2) as g:
            attn(g, True, True)
        attn(ng - 2, True, False)
        attn(ng - 1, False, False)

    @block.tensor
    def _(pe_):
        mm = pe_.matmul
        pe_.wait_ge(A_ready, 1)
        pe_.wait_ge(pool_set, 4)
        for k in range(KP):
            last = mm(b6[:, 0:D], ones, A_sb[:, k, :], start=(k == 0), stop=(k == KP - 1))
        last.then_inc(cs_ps, 1)
        pe_.wait_ge(csum_ready, 1)

        def e_tile(g, i):
            b, c, r = i // 2, i % 2, tile_rows(i)
            if i == 0:
                pe_.wait_ge(qkv_used, at(g, 9, 0))
            if i == 1:
                pe_.wait_ge(parts_ready, at(g, 9, 0))
            if c == 0:
                pe_.wait_ge(pT_in[b], for_dma(g, 1, 1))
            pe_.wait_ge(z_used, at(g, 8, i - 1))
            for k in range(KP):
                last = mm(z_ps[c][0:r, :], pT[:, b, k, c * P:c * P + r], A_sb[:, k, :],
                          start=(k == 0), stop=(k == KP - 1))
            last.then_inc(z_ready, 1)

        def e_stage(g):
            for i in range(2 * GB):
                e_tile(g, i)

        def x_transpose(g, t):
            pe_.wait_ge(xn_ready, at(g, 9, t + 1))
            pe_.wait_ge(xT_in, at(g, 9, t))
            for k in range(2):
                last = pe_.transpose(xT_ps[:, k * P:(k + 1) * P], xn[:, t % 2, k * P:(k + 1) * P], idf[:, :])
            last.then_inc(xT_tr, 1)

        def x_project(g, t):
            pe_.wait_ge(xT_in, at(g, 9, t + 1))
            pe_.wait_ge(qkv_used, at(g, 9, t))
            for k in range(2):
                mm(qk_ps, xTs[:, t % 2, k * P:(k + 1) * P], wqkv[:, k, 0:2 * D], start=(k == 0), stop=(k == 1))
            for k in range(2):
                last = mm(v_ps, xTs[:, t % 2, k * P:(k + 1) * P], wqkv[:, k, 2 * D:3 * D],
                          start=(k == 0), stop=(k == 1))
            last.then_inc(qkv_ready, 1)

        def x_turn(g, t):
            pe_.wait_ge(rope_done, at(g, 9, t + 1))
            pe_.wait_ge(parts_ready, at(g, 9, t))
            for f in range(4):
                last = pe_.transpose(qkT_ps[:, f * P:(f + 1) * P], qks[:, t % 2, f * P:(f + 1) * P], idf[:, :])
            last.then_inc(qkT_ready, 1)

        def run(g):
            for s in range(NT + 3):
                if 1 <= s < NT + 1:
                    x_transpose(g, s - 1)
                if 3 <= s < NT + 3:
                    x_turn(g, s - 3)
                if 1 <= s < NT + 1:
                    x_project(g, s - 1)

        def max_unit(g, qd, u):
            banks = 2 if qd else 4
            pe_.wait_ge(mx_used, at(g, NQ * NMX, qd * NMX + max(u + 1 - banks, 0)))
            q, k = qh[0:KR, qd % 2], kh[0:KR, qd % 2]
            j, t = max_tile(u)
            if t < 2 * GB:
                b = t // 2
                if u % 16 == 0:
                    pe_.wait_ge(hat_in[qd % 2][b // 2], for_dma(g, NHAT, (qd // 2 + 1) * (NHAT // 2)))
                if u == 0:
                    pe_.wait_ge(cv_done, at(g, 3 * NQ, 3 * qd))
                    pe_.wait_ge(ca_done, at(g, 2 * NQ, 2 * qd))
                last = mm(max_bank(qd, u), q[:, j, b * SB_ + t % 2 * P:b * SB_ + (t % 2 + 1) * P],
                          k[:, j, b * SB_:b * SB_ + S], start=True, stop=True)
            else:
                for b in range(GB):
                    last = mm(max_bank(qd, u)[32 * b:32 * b + 32, :], q[:, j, b * SB_ + 2 * P:(b + 1) * SB_],
                              k[:, j, b * SB_:b * SB_ + S], start=True, stop=True)
            last.then_inc(mx_ready, 1)

        def max_turn(g, qd, i):
            if i == 0:
                pe_.wait_ge(cs_ready, at(g, NQ, qd + 1))
            elif i == 4:
                pe_.wait_ge(ca_done, at(g, 2 * NQ, 2 * qd + 1))
            elif i > 1:
                pe_.wait_ge(cv_done, at(g, 3 * NQ, 3 * qd + i - 1))
            dst = b01[KR:KR + PARTS, i % 2 * 512:(i % 2 + 1) * 512].bitcast(BF16)
            for k in range(4 if i == 0 else 2 * GB):
                last = pe_.transpose(dst[:, k * P:(k + 1) * P], cs[:, 2 * GB, k, :] if i == 0 else cs[:, k, i - 1, :],
                                     idb[:, :])
            last.then_inc(ct_ready, 1)

        def score_unit(g, qd, b, j):
            n = (qd * GB + b) * 4 + j
            pe_.wait_ge(p_ready, at(g, 64, n - 1))
            if b == 0:
                if j % 2 == 0:
                    pe_.wait_ge(cv_done, at(g, 3 * NQ, 3 * qd + 2 + j // 2))
                else:
                    pe_.wait_ge(ca_done, at(g, 2 * NQ, 2 * qd + 1 + j // 2))
            q, k = qh[:, qd % 2, j], kh[:, qd % 2, j]
            for c in range(2):
                last = mm(scp[n % 2][:, c, 0:S], k[:, b * SB_ + c * P:b * SB_ + (c + 1) * P],
                          q[:, b * SB_:b * SB_ + S], start=True, stop=True)
            last.then_inc(s_ready, 1)

        def score_rem(g, qd, b):
            m = qd * GB + b
            pe_.wait_ge(pr_ready, at(g, 16, m))
            for j in range(4):
                last = mm(b6[32 * j:32 * j + 32, 0:S], kh[:, qd % 2, j, b * SB_ + 2 * P:(b + 1) * SB_],
                          qh[:, qd % 2, j, b * SB_:b * SB_ + S], start=True, stop=True)
            last.then_inc(r_ready, 1)

        def value_unit(g, qd, b, c):
            m = qd * GB + b
            if c == 0:
                pe_.wait_ge(p_ready, at(g, 64, 4 * m + 4))
                pe_.wait_ge(o_used, at(g, 16, m))
            if c < 2:
                for j in range(4):
                    n = 4 * m + j
                    v0 = ((2 * b + c) * H + 4 * qd + j) * (DH + 1)
                    last = mm(b7[HP * j:HP * (j + 1), 0:S], Vflat[:, v0:v0 + HP], prob[:, n % PRING, c, :],
                              start=(c == 0), stop=False, skip_group_check=True)
                if c == 1:
                    last.then_inc(pv_done, 1)
            else:
                pe_.wait_ge(pr_ready, at(g, 16, m + 1))
                mm(b7[:, 0:S], Vbd[:, b, qd, :], probr[:, m % 2, :], start=False, stop=True, skip_group_check=True
                   ).then_inc(av_ready, 1)

        def first_maxima(g, tiles):
            if len(tiles) and tiles[0] == 0:
                pe_.wait_ge(xT_in, at(g, 9, 9))
                pe_.wait_ge(qkv_used, at(g, 9, 9))
                pe_.wait_ge(wo_used, at(g, 9, 0))
                pe_.wait_ge(an_ready, at(g, 9, 0))
            for u in tiles:
                max_unit(g, 0, u)

        def attn(g, nxt, emb):
            for i in range(5):
                max_turn(g, 0, i)
            pe_.wait_ge(parts_ready, at(g, 9, 9))
            for s_ in (aT_in, wo_used, yT_in, an_ready):
                pe_.wait_ge(s_, at(g, 9, 0))
            pe_.wait_ge(z_used, at(g + 1, 8, 8) if nxt else at(g + 1, 8, 0))
            pe_.wait_ge(slot_ready, at(g, 1, 0))
            pe_.wait_ge(vbd_ready, at(g, 1, 1))
            for qd in range(NQ):
                pe_.wait_ge(p_ready, at(g, 64, 16 * qd - 1))
                for _ in range(NWARM if qd else NWARM0):
                    mm(scp[0][:, 0, :], idf[:, :], wqkv[:, 0, 0:512], start=True, stop=True)
                for b in range(GB):
                    for j in range(4):
                        score_unit(g, qd, b, j)
                        if qd + 1 < NQ and b < GB - 1:
                            for i in range(NMX // (4 * (GB - 1))):
                                max_unit(g, qd + 1, (4 * b + j) * (NMX // (4 * (GB - 1))) + i)
                        if b >= 1 and j < 3:
                            value_unit(g, qd, b - 1, j)
                    if qd + 1 < NQ and b == GB - 1:
                        max_turn(g, qd + 1, 0)
                        max_turn(g, qd + 1, 1)
                    score_rem(g, qd, b)
                for c in range(3):
                    value_unit(g, qd, GB - 1, c)
                    if qd + 1 < NQ:
                        max_turn(g, qd + 1, 2 + c)
            pe_.wait_ge(cv_done, at(g, 3 * NQ, 3 * NQ))
            pe_.wait_ge(ca_done, at(g, 2 * NQ, 2 * NQ))
            pe_.wait_ge(p_ready, at(g, 64, 64))
            pe_.wait_ge(pr_ready, at(g, 16, 16))
            for s in range(NT + 7):
                if emb and s >= TAIL:
                    tiles = MAX_STEPS.get(s, ())
                    for c in range(2):
                        if s > TAIL or c:
                            e_tile(g + 2, 2 * (s - TAIL) + c)
                        first_maxima(g + 1, tiles[4 * c:4 * c + 4])
                elif nxt and s in MAX_STEPS:
                    first_maxima(g + 1, MAX_STEPS[s])
                if nxt and 1 <= s < NT + 1:
                    x_transpose(g + 1, s - 1)
                if s < NT:
                    t = s
                    if t == 0:
                        pe_.wait_ge(o_used, at(g, 16, 16))
                    pe_.wait_ge(an_ready, at(g, 9, t))
                    for qd in range(NQ):
                        last = pe_.transpose(oT_ps[:, qd * P:(qd + 1) * P], O_sb[:, qd, t * P:(t + 1) * P], idf[:, :])
                    last.then_inc(oT_ready, 1)
                if 1 <= s < NT + 1:
                    t = s - 1
                    pe_.wait_ge(an_ready, at(g, 9, t + 1))
                    pe_.wait_ge(aT_in, at(g, 9, t))
                    pe_.wait_ge(yT_in, at(g, 9, t - 5))
                    for k in range(2):
                        last = pe_.transpose(aT_ps[:, k * P:(k + 1) * P],
                                             an[:, 8 * k:8 * k + 8, :].rearrange("p h d -> p (h d)"), idf[:, :])
                    last.then_inc(aT_ready, 1)
                if 6 <= s < NT + 6:
                    t = s - 6
                    pe_.wait_ge(y_ready, at(g, 9, t + 1))
                    pe_.wait_ge(yT_in, at(g, 9, t))
                    pe_.wait_ge(aT_in, at(g, 9, min(t + 6, NT)))
                    for k in range(2):
                        last = pe_.transpose(yT_ps[:, k * P:(k + 1) * P], y[:, t % 2, k * P:(k + 1) * P], idf[:, :])
                    last.then_inc(yT_ready, 1)
                if nxt and 3 <= s < NT + 3:
                    x_turn(g + 1, s - 3)
                if nxt and 1 <= s < NT + 1:
                    x_project(g + 1, s - 1)
                if 1 <= s < NT + 1:
                    t = s - 1
                    pe_.wait_ge(aT_in, at(g, 9, t + 1))
                    pe_.wait_ge(wo_used, at(g, 9, t))
                    for k in range(2):
                        last = mm(wo_ps, aTs[:, k * P:(k + 1) * P], wo[:, k, :], start=(k == 0), stop=(k == 1))
                    last.then_inc(wo_ready, 1)
                if 6 <= s < NT + 6:
                    t = s - 6
                    pe_.wait_ge(yT_in, at(g, 9, t + 1))
                    for k in range(2):
                        last = mm(lg_ps[:, t, :], yTs[:, k * P:(k + 1) * P], wr[:, k, :], start=(k == 0), stop=(k == 1))
                    last.then_inc(lg_ready, 1)
                if emb and s == TAIL - 1:
                    e_tile(g + 2, 0)
            pe_.wait_ge(oh_ready, at(g, 1, 1))
            mm(rk_ps, before[:, :], ohb[:, :, :].rearrange("p t e -> p (t e)"), start=True, stop=False,
               skip_group_check=True)
            mm(rk_ps, onesb[:, :], ctb[:, :, :].rearrange("p t e -> p (t e)"), start=False, stop=False,
               skip_group_check=True)
            for b in range(GB):
                mm(rk_ps[:, 2 * GB * NE:NT * NE], fromb[:, b, :], pairb[:, b, :], start=False, stop=(b == GB - 1),
                   skip_group_check=True)
            mm(tot_ps, onesb[:, :], totb[:, :], start=True, stop=True).then_inc(rk_ready, 1)
            if nxt:
                first_maxima(g + 1, range(M0, NMX))

        e_stage(0)
        run(0)
        first_maxima(0, range(NMX))
        e_stage(1)
        with pe_.Fori(0, ng - 2) as g:
            attn(g, True, True)
        attn(ng - 2, True, False)
        attn(ng - 1, False, False)

    ctx.close()


def phase_b(nc, sem, cap, ntok, chunk, cuts, xe, W1, W2, out_rows):
    ctx = ExitStack()

    def sb(name, shape, dt=F32):
        return ctx.enter_context(nc.sbuf_tensor(name, shape, dt))

    nch = cap // chunk
    UN = 2 * nch
    RB = 3 if UN % 3 == 0 else 2
    KF = FF // P
    NC = len(cuts)
    WC = 8
    PRODUCTS = ((0, 0), (1, 0), (0, 1))
    offs = [sum(cuts[:i]) for i in range(NC)]
    WN = 2 * FF + KF * D
    w_raw = sb("w_raw", [P, WN])
    w_cut = [[sb(f"w_cut{i}{b}", [P, WN], F32R) for b in range(2)] for i in range(2)]
    w1 = [[w[:, 0:2 * FF].rearrange("p (k n) -> p k n", k=2) for w in ws] for ws in w_cut]
    w2 = [[w[:, 2 * FF:WN].rearrange("p (k n) -> p k n", k=KF) for w in ws] for ws in w_cut]
    rows = sb("rows", [P, RB, NC, ROW])
    yb = sb("yb", [P, 2, NC, D])
    yT = [sb(f"yT{i}", [P, 2, 2, chunk], F32R) for i in range(2)]
    hT = [sb(f"hT{i}", [P, 2, KF, chunk], F32R) for i in range(2)]
    ob = sb("ob", [P, RB, NC, D])
    idx = sb("idx", [P, RB, NC], U32)
    idf = sb("idf2", [P, P])

    def bank(name):
        return ctx.enter_context(nc.psum_tensor(name, [P, 512], F32))

    yT_ps = [bank(f"yTp{k}") for k in range(2)]
    h_ps = [bank(f"hp{k}") for k in range(4)]
    o_ps = [bank(f"op{k}") for k in range(2)]

    credit = []

    def csem(name, dma=False):
        s = sem(name)
        credit.append((s, dma))
        return s

    w_in = csem("w_in", 1)
    w_high, w_ready = csem("w_high"), csem("w_ready")
    rows_in = [csem(f"rows_in{i}", 1) for i in range(RB)]
    ow = sem("ow")
    scattered = csem("out_scattered")
    id_ready, id_zero, settled = sem("id_ready"), sem("id_zero"), sem("out_settled")
    yb_ready, yT_tr = csem("yb_ready"), csem("yT_tr")
    yT_high, yT_sb = csem("yT_high"), csem("yT_sb")
    h_ready = csem("h_ready")
    h_high, h_cut = csem("h_high"), csem("h_cut")
    o_ready, ob_ready = csem("o_ready"), csem("ob_ready")
    block = ctx.enter_context(nc.Block())

    @block.sync
    def _(sp):
        for s, dma in credit:
            sp.sem_inc(s, 16 if dma else 1)
        def weights(expert):
            sp.dma_start(w_raw[:, 0:2 * FF].rearrange("p (k n) -> p k n", k=2),
                         W1[bass.ds(expert, 1), :, :].rearrange("a (k p) n -> p (a k) n", p=P)).then_inc(w_in, 16)
            sp.dma_start(w_raw[:, 2 * FF:WN].rearrange("p (k n) -> p k n", k=KF),
                         W2[bass.ds(expert, 1), :, :].rearrange("a (k p) n -> p (a k) n", p=P)).then_inc(w_in, 16)

        def pair(e2, last):
            for c in range(UN):
                sp.wait_ge(ob_ready, at(e2, UN * NC, (c - RB + 1) * NC if c >= RB else 0))
                settle(sp, settled)
                for i in range(NC):
                    sp.dma_start(rows[0:cuts[i], c % RB, i, :],
                                 xe[bass.ds(e2 * (2 * cap) + (c * chunk + offs[i]), cuts[i]), :]).then_inc(rows_in[c % RB], 16)
                if c % nch == 0 and not (last and c == nch):
                    sp.wait_ge(w_ready, at(e2, 2 * WC, (c // nch + 1) * WC))
                    settle(sp, settled)
                    weights(e2 * 2 + c // nch + 1)

        weights(0)
        with sp.Fori(0, NE // 2 - 1) as e2:
            pair(e2, False)
        pair(NE // 2 - 1, True)

    @block.gpsimd
    def _(pool):
        def cut_weights(e2, e, done):
            for i in range(WC):
                cols = slice(i * WN // WC, (i + 1) * WN // WC)
                if i == 0:
                    pool.wait_ge(w_in, 16 * at(e2, 4, 2 * e + 2))
                    pool.wait_ge(o_ready, done)
                    settle(pool, settled)
                pool.tensor_scalar(w_cut[0][e][:, cols], w_raw[:, cols], 1.0, 1.0, ALU.mult, ALU.mult
                                   ).then_inc(w_high, 1)
                pool.wait_ge(w_high, at(e2, 2 * WC, e * WC + i + 1))
                pool.tensor_tensor(w_cut[1][e][:, cols], w_raw[:, cols], w_cut[0][e][:, cols], ALU.subtract
                                   ).then_inc(w_ready, 1)

        pool.memset(idf[:, :], 0.0).then_inc(id_zero, 1)
        pool.wait_ge(id_zero, 1)
        pool.affine_select(out=idf[:, :], in_=idf[:, :], compare_op=ALU.not_equal, fill=1.0, base=0,
                           pattern=[[-1, P]], channel_multiplier=1).then_inc(id_ready, 1)
        def pair(e2, last):
            for c in range(UN):
                if c % nch == 1 and not (last and c > nch):
                    done = at(e2, UN * NC, c // nch * nch * NC)
                    if c < nch:
                        cut_weights(e2, 1, done)
                    else:
                        cut_weights(e2 + 1, 0, done)
                pool.wait_ge(ob_ready, at(e2, UN * NC, (c + 1) * NC))
                settle(pool, settled)
                for i in range(NC):
                    pool.indirect_dma_start(
                        out=out_rows, out_offset=bass.IndirectOffsetOnAxis(ap=idx[0:cuts[i], c % RB, i:i + 1], axis=0),
                        in_=ob[0:cuts[i], c % RB, i, :], in_offset=None, bounds_check=ntok - 1,
                        oob_is_err=False).then_inc(ow, 16)
                pool.wait_ge(ow, 16 * NC * (e2 * UN + (c + 1)))
                pool.sem_inc(scattered, 1)

        cut_weights(0, 0, at(0, UN * NC, 0))
        with pool.Fori(0, NE // 2 - 1) as e2:
            pair(e2, False)
        pair(NE // 2 - 1, True)

    @block.vector
    def _(dve):
        def norm(e2, c):
            dve.wait_ge(rows_in[c % RB], 16 * at(e2, UN * NC // RB, (c // RB + 1) * NC))
            dve.wait_ge(yT_tr, at(e2, UN, c - 1))
            for i in range(NC):
                n = cuts[i]
                r = rows[0:n, c % RB, i, :]
                last = dve.tensor_scalar(yb[0:n, c % 2, i, :], r[:, 0:D], r[:, D:D + 1], r[:, D + 1:D + 2],
                                         ALU.subtract, ALU.mult)
            last.then_inc(yb_ready, 1)

        def turn_rest(e2, c):
            dve.wait_ge(yT_high, at(e2, UN, c + 1))
            for k in range(2):
                last = dve.tensor_tensor(yT[1][:, c % 2, k, :], yT_ps[k][:, 0:chunk], yT[0][:, c % 2, k, :],
                                         ALU.subtract)
            last.then_inc(yT_sb, 1)

        def relu_rest(e2, c, f):
            dve.wait_ge(h_high, at(e2, UN * KF, c * KF + f + 1))
            dve.scalar_tensor_tensor(hT[1][:, c % 2, f, :], h_ps[f % 4][:, 0:chunk], 0.0, hT[0][:, c % 2, f, :],
                                     ALU.max, ALU.subtract).then_inc(h_cut, 1)

        def result(e2, c, i):
            n = cuts[i]
            r = rows[0:n, c % RB, i, :]
            if i == 0:
                dve.wait_ge(scattered, at(e2, UN, c - RB + 1 if c >= RB else 0))
            dve.wait_ge(o_ready, at(e2, UN * NC, c * NC + i + 1))
            dve.tensor_copy(idx[0:n, c % RB, i:i + 1], r[:, D + 3:D + 4])
            dve.scalar_tensor_tensor(ob[0:n, c % RB, i, :], o_ps[i % 2][0:n, 0:D], r[:, D + 2:D + 3], r[:, 0:D],
                                     ALU.mult, ALU.add).then_inc(ob_ready, 1)

        with dve.Fori(0, NE // 2) as e2:
            norm(e2, 0)
            turn_rest(e2, 0)
            for c in range(UN):
                if c + 1 < UN:
                    norm(e2, c + 1)
                for f in range(KF):
                    relu_rest(e2, c, f)
                    if f == 3 and c + 1 < UN:
                        turn_rest(e2, c + 1)
                for i in range(NC):
                    result(e2, c, i)

    @block.scalar
    def _(act):
        def turn(e2, c):
            act.wait_ge(yT_tr, at(e2, UN, c + 1))
            act.wait_ge(h_ready, at(e2, UN * KF, (c - 1) * KF if c >= 2 else 0))
            act.activation(yT[0][:, c % 2, 0, :], yT_ps[0][:, 0:chunk], ACT.Copy)
            act.activation(yT[0][:, c % 2, 1, :], yT_ps[1][:, 0:chunk], ACT.Copy).then_inc(yT_high, 1)

        with act.Fori(0, NE // 2) as e2:
            turn(e2, 0)
            for c in range(UN):
                for f in range(KF):
                    act.wait_ge(h_ready, at(e2, UN * KF, c * KF + f + 1))
                    if f == 0:
                        act.wait_ge(o_ready, at(e2, UN * NC, (c - 1) * NC if c >= 2 else 0))
                    act.activation(hT[0][:, c % 2, f, :], h_ps[f % 4][:, 0:chunk], ACT.Relu).then_inc(h_high, 1)
                    if f == 3 and c + 1 < UN:
                        turn(e2, c + 1)

    @block.tensor
    def _(pe_):
        mm = pe_.matmul
        pe_.wait_ge(id_ready, 1)

        def turn(e2, c):
            pe_.wait_ge(yb_ready, at(e2, UN, c + 1))
            pe_.wait_ge(yT_sb, at(e2, UN, c))
            for i in range(NC):
                n = cuts[i]
                for k in range(2):
                    last = pe_.transpose(yT_ps[k][:, offs[i]:offs[i] + n], yb[0:n, c % 2, i, k * P:(k + 1) * P],
                                         idf[0:n, 0:n])
            last.then_inc(yT_tr, 1)

        with pe_.Fori(0, NE // 2) as e2:
            turn(e2, 0)
            for c in range(UN):
                e = c // nch
                if c % nch == 0:
                    pe_.wait_ge(w_ready, at(e2, 2 * WC, (e + 1) * WC))
                pe_.wait_ge(yT_sb, at(e2, UN, c + 1))
                for f in range(KF):
                    pe_.wait_ge(h_cut, at(e2, UN * KF, c * KF + f - 3))
                    for k in range(2):
                        for i, j in PRODUCTS:
                            last = mm(h_ps[f % 4][:, 0:chunk], w1[i][e][:, k, f * P:(f + 1) * P], yT[j][:, c % 2, k, :],
                                      start=(k == 0 and i == j), stop=(k == 1 and j == 1))
                    last.then_inc(h_ready, 1)
                    if f == 1 and c + 1 < UN:
                        turn(e2, c + 1)
                for i in range(NC):
                    m = c * NC + i
                    pe_.wait_ge(ob_ready, at(e2, UN * NC, m - 1))
                    for f in range(KF):
                        if i == 0:
                            pe_.wait_ge(h_cut, at(e2, UN * KF, c * KF + f + 1))
                        for a, b in PRODUCTS:
                            last = mm(o_ps[i % 2][0:cuts[i], 0:D], hT[a][:, c % 2, f, offs[i]:offs[i] + cuts[i]],
                                      w2[b][e][:, f, :], start=(f == 0 and a == b), stop=(f == KF - 1 and b == 1))
                    last.then_inc(o_ready, 1)

    ctx.close()


def host_constants():
    dim4 = D // 4
    yy, xx = np.meshgrid(np.arange(HW, dtype=np.float32), np.arange(HW, dtype=np.float32), indexing="ij")
    omega = (1.0 / (np.float32(10000.0) ** (np.arange(dim4, dtype=np.float32) / (dim4 - 1)))).astype(np.float32)
    ya, xa = yy.reshape(-1)[:, None] * omega[None, :], xx.reshape(-1)[:, None] * omega[None, :]
    pos = np.concatenate([np.sin(xa), np.cos(xa), np.sin(ya), np.cos(ya)], axis=1).astype(np.float32)
    pe = np.zeros((P, 2, D), np.float32)
    pe[:, 0] = pos[:P]
    pe[:IMG1, 1] = pos[P:]
    inv = (1.0 / np.float32(10000.0) ** (np.arange(0, DH, 2, dtype=np.float32) / DH)).astype(np.float32)
    where = np.stack([np.arange(P), P + np.arange(P), 2 * P + np.arange(P) % 32]).astype(np.float32)
    ang = (where[:, :, None] * inv).astype(np.float32)
    rope = np.stack([np.cos(ang), np.sin(ang)]).astype(np.float32)
    rope = np.ascontiguousarray(rope.transpose(2, 0, 1, 3))
    row = np.arange(P)
    valid = (row % 32 < REM).astype(np.float32)
    masks = np.zeros((P, 24), np.float32)
    masks[:, 0] = valid
    for b in range(1, GB):
        masks[:, b] = valid * (row < 32 * b)
    masks[:, 4] = (1 - valid) * BIG
    masks[:, 8:16] = np.arange(NE)
    tokens = np.zeros((P, NT), np.float32)
    for t in range(2 * GB):
        tokens[:, t] = (t // 2) * S + (t % 2) * P + row
    tokens[:, 2 * GB] = (row // 32) * S + 2 * P + row % 32
    return pe, rope, masks, tokens


_ORDER = ["patches_tok", "patches_T", "txt", "ln1_w", "WT", "ln2_w", "Wqkv", "bqkv", "Wo", "bo",
          "gamma", "beta", "Wr", "W1", "W2", "pe", "rope", "masks", "tokens"]


def lay_out(i):
    x = np.asarray(i["x"])
    nb = x.shape[0]
    p = x.reshape(nb, 3, HW, 16, HW, 16).transpose(0, 2, 4, 1, 3, 5).reshape(nb, NIMG, PD)
    order = np.concatenate([np.arange(0, DH, 2), np.arange(1, DH, 2)])
    cols = (np.arange(4)[:, None, None] * P + order[None, :, None] + np.arange(H // 2)[None, None, :] * DH).reshape(-1)
    cols = np.concatenate([cols, np.arange(2 * D, 3 * D)])
    pe, rope, masks, tokens = host_constants()
    a = {
        "patches_tok": p, "patches_T": p.reshape(nb, NIMG, KP, P).transpose(0, 3, 2, 1),
        "txt": i["txt"], "ln1_w": np.asarray(i["L0_tok_ln1_w"]).reshape(KP, P).T, "WT": np.asarray(i["L0_tok_W"]).T,
        "ln2_w": i["L0_tok_ln2_w"], "Wqkv": np.asarray(i["L0_attn_Wqkv"])[:, cols],
        "bqkv": np.asarray(i["L0_attn_bqkv"])[cols], "Wo": i["L0_attn_Wo"], "bo": i["L0_attn_bo"],
        "gamma": i["L0_attn_gamma"], "beta": i["L0_attn_beta"], "Wr": i["L0_ffn_Wr"],
        "W1": i["L0_ffn_W1"], "W2": i["L0_ffn_W2"], "pe": pe, "rope": rope, "masks": masks, "tokens": tokens,
    }
    return {k: np.ascontiguousarray(np.asarray(a[k])) for k in _ORDER}


def kernel(**inputs):
    import concourse.bacc as bacc
    from concourse.bass_utils import run_bass_kernel_spmd as run
    arrays = lay_out(inputs)
    nb = arrays["txt"].shape[0]
    nc = bacc.Bacc("TRN2", target_bir_lowering=False, num_devices=1)
    args = [nc.dram_tensor("in_" + k, arrays[k].shape, mybir.dt.from_np(arrays[k].dtype),
                           kind="ExternalInput").ap() for k in _ORDER]
    out = nc.dram_tensor("out_0", (nb, S, D), F32, kind="ExternalOutput").ap()
    build_program(nc, nb, 364, (122, 121, 121), *args, out)
    r = run(nc, [{"in_" + k: v for k, v in arrays.items()}], core_ids=[0])
    return r.results[0]["out_0"]
```
